# Optimizing a Trainium2 kernel written in Bass

```python
import numpy as np
import jax
import jax.numpy as jnp

def _softmax(x, axis=-1):
    return jax.nn.softmax(x, axis=axis)

def _gelu(x):
    return jax.nn.gelu(x, approximate=True)

def _silu(x):
    return jax.nn.silu(x)

def _sigmoid(x):
    return jax.nn.sigmoid(x)

def _layernorm(x, axis=-1, eps=1e-05):
    m = jnp.mean(x, axis=axis, keepdims=True)
    v = jnp.var(x, axis=axis, keepdims=True)
    return (x - m) / jnp.sqrt(v + eps)

def _scatter_add(tgt, idx, src, axis=0):
    return tgt.at[idx].add(src)

def _segment_sum(src, seg, n):
    return jax.ops.segment_sum(src, seg, n)
kernel_name = 'mk_adj_resnorm_d2_adj_r2_e33d61'

def setup_inputs(seed: int=0):
    np.random.seed(seed)
    _w = jnp.asarray

    def _rec_inputs():
        import jax
        import jax.numpy as jnp
        _gk = jax.random.key(seed)
        x = -0.0002928 + 1 * jax.random.normal(jax.random.fold_in(_gk, 1), (1354, 256), jnp.float32)
        _a = jax.random.bernoulli(jax.random.fold_in(_gk, 2), 0.00295421, (1354, 1354))
        adj = _a.astype(jnp.int32)
        return (x, adj)
    x, adj = _rec_inputs()

    def _L0_gnn_setup():
        import jax, jax.numpy as jnp
        import numpy as np
        N = 4096
        F_IN = 256
        F_OUT = 256
        key = jax.random.key(seed)
        k1, k2, k3 = jax.random.split(key, 3)
        X = jax.random.normal(k1, (N, F_IN), dtype=jnp.float32)
        adj = jax.random.randint(k2, (N, N), 0, 2, dtype=jnp.int32)
        limit = float(np.sqrt(6.0 / (F_IN + F_OUT)))
        weight = jax.random.uniform(k3, (F_IN, F_OUT), minval=-limit, maxval=limit, dtype=jnp.float32)
        return {'X': X, 'adj': adj, 'weight': weight}
    _L0_gnn_all = _L0_gnn_setup()
    _L0_gnn_in = {k: v for k, v in _L0_gnn_all.items() if k in ('weight',)}
    del _L0_gnn_all

    def _L1_gnn_setup():
        import jax, jax.numpy as jnp
        import numpy as np
        N = 2048
        STATE_DIM = 256
        OUTPUT_DIM = 256
        N_STEPS = 5
        W_STD = 0.02

        def _lin_params(key, out_dim, in_dim):
            W = jax.random.normal(key, (out_dim, in_dim), dtype=jnp.float32) * W_STD
            b = jnp.zeros((out_dim,), dtype=jnp.float32)
            return (W, b)
        key = jax.random.key(seed)
        ks = jax.random.split(key, 10)
        prop_state = jax.random.normal(ks[0], (N, STATE_DIM), dtype=jnp.float32)
        A = jax.random.randint(ks[1], (N, N), 0, 2, dtype=jnp.int64)
        in_W, in_b = _lin_params(ks[2], STATE_DIM, STATE_DIM)
        out_W, out_b = _lin_params(ks[3], STATE_DIM, STATE_DIM)
        r_W, r_b = _lin_params(ks[4], STATE_DIM, 3 * STATE_DIM)
        z_W, z_b = _lin_params(ks[5], STATE_DIM, 3 * STATE_DIM)
        h_W, h_b = _lin_params(ks[6], STATE_DIM, 3 * STATE_DIM)
        o1_W, o1_b = _lin_params(ks[7], STATE_DIM, STATE_DIM)
        o2_W, o2_b = _lin_params(ks[8], OUTPUT_DIM, STATE_DIM)
        return {'prop_state': prop_state, 'A': A, 'in_W': in_W, 'in_b': in_b, 'out_W': out_W, 'out_b': out_b, 'r_W': r_W, 'r_b': r_b, 'z_W': z_W, 'z_b': z_b, 'h_W': h_W, 'h_b': h_b, 'o1_W': o1_W, 'o1_b': o1_b, 'o2_W': o2_W, 'o2_b': o2_b}
    _L1_gnn_all = _L1_gnn_setup()
    _L1_gnn_in = {k: v for k, v in _L1_gnn_all.items() if k in ('in_W', 'in_b', 'out_W', 'out_b', 'r_W', 'r_b', 'z_W', 'z_b', 'h_W', 'h_b', 'o1_W', 'o1_b', 'o2_W', 'o2_b')}
    del _L1_gnn_all
    return {'x': x, 'adj': adj, 'L0_gnn_weight': _L0_gnn_in['weight'], 'L1_gnn_in_W': _L1_gnn_in['in_W'], 'L1_gnn_in_b': _L1_gnn_in['in_b'], 'L1_gnn_out_W': _L1_gnn_in['out_W'], 'L1_gnn_out_b': _L1_gnn_in['out_b'], 'L1_gnn_r_W': _L1_gnn_in['r_W'], 'L1_gnn_r_b': _L1_gnn_in['r_b'], 'L1_gnn_z_W': _L1_gnn_in['z_W'], 'L1_gnn_z_b': _L1_gnn_in['z_b'], 'L1_gnn_h_W': _L1_gnn_in['h_W'], 'L1_gnn_h_b': _L1_gnn_in['h_b'], 'L1_gnn_o1_W': _L1_gnn_in['o1_W'], 'L1_gnn_o1_b': _L1_gnn_in['o1_b'], 'L1_gnn_o2_W': _L1_gnn_in['o2_W'], 'L1_gnn_o2_b': _L1_gnn_in['o2_b']}

def reference(x, adj, L0_gnn_weight, L1_gnn_in_W, L1_gnn_in_b, L1_gnn_out_W, L1_gnn_out_b, L1_gnn_r_W, L1_gnn_r_b, L1_gnn_z_W, L1_gnn_z_b, L1_gnn_h_W, L1_gnn_h_b, L1_gnn_o1_W, L1_gnn_o1_b, L1_gnn_o2_W, L1_gnn_o2_b):
    import jax
    import jax.numpy as jnp

    def _L0_gnn_ref(X, adj, weight):
        import jax, jax.numpy as jnp
        import numpy as np
        N = 4096
        F_IN = 256
        F_OUT = 256
        a = adj.astype(X.dtype)
        support = a.T @ X
        out = support @ weight
        in_degree = a.sum(axis=0)
        norm = jnp.clip(in_degree, 1.0, None) ** (-0.5)
        out = out * norm[:, None]
        return jax.nn.relu(out)

    def _L1_gnn_ref(prop_state, A, in_W, in_b, out_W, out_b, r_W, r_b, z_W, z_b, h_W, h_b, o1_W, o1_b, o2_W, o2_b):
        import jax, jax.numpy as jnp
        import numpy as np
        N = 2048
        STATE_DIM = 256
        OUTPUT_DIM = 256
        N_STEPS = 5
        W_STD = 0.02

        def _lin_params(key, out_dim, in_dim):
            W = jax.random.normal(key, (out_dim, in_dim), dtype=jnp.float32) * W_STD
            b = jnp.zeros((out_dim,), dtype=jnp.float32)
            return (W, b)
        Af = A.astype(prop_state.dtype)
        AfT = Af.T
        state = prop_state
        for _ in range(N_STEPS):
            s_in = state @ in_W.T + in_b
            s_out = state @ out_W.T + out_b
            a_in = Af @ s_in
            a_out = AfT @ s_out
            a = jnp.concatenate([a_in, a_out, state], axis=-1)
            r = jax.nn.sigmoid(a @ r_W.T + r_b)
            z = jax.nn.sigmoid(a @ z_W.T + z_b)
            joined = jnp.concatenate([a_in, a_out, r * state], axis=-1)
            h_hat = jnp.tanh(joined @ h_W.T + h_b)
            state = (1.0 - z) * state + z * h_hat
        out = jnp.tanh(state @ o1_W.T + o1_b) @ o2_W.T + o2_b
        return out
    x = _layernorm(x + _L0_gnn_ref(x, adj, L0_gnn_weight), axis=-1)
    x = _layernorm(x + _L1_gnn_ref(x, adj, L1_gnn_in_W, L1_gnn_in_b, L1_gnn_out_W, L1_gnn_out_b, L1_gnn_r_W, L1_gnn_r_b, L1_gnn_z_W, L1_gnn_z_b, L1_gnn_h_W, L1_gnn_h_b, L1_gnn_o1_W, L1_gnn_o1_b, L1_gnn_o2_W, L1_gnn_o2_b), axis=-1)
    return x

_drawn_inputs = setup_inputs


def setup_inputs(seed=0):
    import zlib

    import numpy as np

    out = dict(_drawn_inputs(seed))
    spreads = {'L1_gnn_in_b': (0.0, 0.525),
     'L1_gnn_out_b': (0.0, 0.539),
     'L1_gnn_r_b': (0.0, 0.8),
     'L1_gnn_z_b': (0.0, 0.8),
     'L1_gnn_h_b': (0.0, 0.776),
     'L1_gnn_o1_b': (0.0, 0.1),
     'L1_gnn_o2_b': (0.0, 0.1)}
    factors = {'L1_gnn_in_W': 5.812, 'L1_gnn_out_W': 6.115, 'L1_gnn_r_W': 8.0, 'L1_gnn_z_W': 8.0}
    for name, (base, spread) in spreads.items():
        noise = np.random.default_rng([zlib.crc32(name.encode()), seed]).standard_normal(out[name].shape)
        drawn = base * np.exp(spread * noise) if base else spread * noise
        out[name] = jnp.asarray(drawn.astype(out[name].dtype))
    for name, factor in factors.items():
        out[name] = (out[name] * factor).astype(out[name].dtype)
    return out
```

```python
from contextlib import ExitStack

import concourse.bass as bass
from concourse import mybir

ALU = mybir.AluOpType
ACT = mybir.ActivationFunctionType
AX_X = mybir.AxisListType.X
F32 = mybir.dt.float32
F16 = mybir.dt.float16
BF16 = mybir.dt.bfloat16

P = 128
STEPS = 5
EPS = 1e-5
LO = 2048.0
WS = 1024.0


def gated_graph_net(nc: bass.Bass, x, adj, w0, in_W, in_b, out_W, out_b, r_W, r_b, z_W, z_b,
                    h_W, h_b, o1_W, o1_b, o2_W, o2_b, out):
    N, D = x.shape
    NC = -(-N // P)
    NF = N // P
    H = D // P
    TW = 512
    TILES = [(a, min(TW, N - a)) for a in range(0, N, TW)]
    NT = len(TILES)
    CPT = TW // P
    KC = 3 * H
    M6 = 3 * H
    G = M6 * P
    assert H == 2 and NT == 3 and r_W.shape == (D, 3 * D)

    def rows(c):
        return min(P, N - c * P)

    def chunks(t):
        return range(t * CPT, min((t + 1) * CPT, NC))

    def column_runs(t):
        c0, c1 = chunks(t)[0], chunks(t)[-1] + 1
        return [(P, c0, min(c1, NF))] + ([(rows(NF), NF, c1)] if c1 > NF else [])

    with ExitStack() as ctx:
        def sb(name, shape, dt=F32):
            return ctx.enter_context(nc.sbuf_tensor(name, shape, dt))

        def sem(name):
            return ctx.enter_context(nc.semaphore(name))

        A = sb("A", [P, NC, N], F16)
        AT = sb("AT", [P, NC, N], F16)
        X = sb("X", [P, NC, D])
        SnH = sb("SnH", [P, NC, D], F16)
        SnL = sb("SnL", [P, NC, D], F16)
        Sm = sb("Sm", [P, H, N])
        Wh = sb("Wh", [P, KC, G], F16)
        Wl = sb("Wl", [P, KC, G], F16)
        Wp = sb("Wp", [P, KC, G], F16)
        Oh = sb("Oh", [P, 2 * H, D], F16)
        Ol = sb("Ol", [P, 2 * H, D], F16)
        Op = sb("Op", [P, 2 * H, D], F16)
        ident = sb("ident", [P, P])
        ident16 = sb("ident16", [P, P], F16)
        ones16 = sb("ones16", [P, 1], F16)
        b_in = sb("b_in", [P, 2, H])
        b_gate = sb("b_gate", [P, M6])
        b_o1 = sb("b_o1", [P, H])
        b_o2 = sb("b_o2", [P, D])
        v_gate = sb("v_gate", [P, 2, M6])
        rdeg = sb("rdeg", [P, NC])
        cdeg = sb("cdeg", [P, NC])
        norm = sb("norm", [P, NC])
        stats = sb("stats", [P, NC, 6])
        mv = sb("mv", [P, NC, 2])
        rstd = sb("rstd", [P, NC])
        eps = sb("eps", [P, 1])
        relu = sb("relu", [P, 4, D])
        c32 = sb("c32", [P, 2, G])

        uv = sb("uv", [P, 4 * N])
        UVH = uv[:, 0:2 * N].bitcast(F16).rearrange("p (k n) -> p k n", k=2 * H)
        UVL = uv[:, 2 * N:4 * N].bitcast(F16).rearrange("p (k n) -> p k n", k=2 * H)
        gates_raw = uv[:, 0:3 * H * 3 * D].rearrange("p (k m) -> p k m", k=3 * H)
        Tm = uv[:, 0:2 * N].rearrange("p (k n) -> p k n", k=H)
        TH = uv[:, 2 * N:3 * N].bitcast(F16).rearrange("p (k n) -> p k n", k=H)
        TL = uv[:, 3 * N:4 * N].bitcast(F16).rearrange("p (k n) -> p k n", k=H)

        act_mem = sb("act_mem", [P, max(4 * H * TW, 3 * NC * D // 2)])
        gR, gZ, gH = (act_mem[:, q * H * TW:(q + 1) * H * TW].rearrange("p (k n) -> p k n", k=H)
                      for q in range(3))
        rs_mem = act_mem[:, 3 * H * TW:4 * H * TW].bitcast(F16).rearrange("p (s k n) -> p s k n", s=2, k=H)
        rsH, rsL = rs_mem[:, 0], rs_mem[:, 1]
        Y = act_mem[:, 0:3 * NC * D // 2].bitcast(BF16).rearrange("p (s c d) -> p s c d", s=3, c=NC)

        gt_mem = sb("gt_mem", [P, 4 * G])
        gT = gt_mem[:, :].rearrange("p (k g) -> p k g", k=4)
        XB = gt_mem[:, 0:NC * D].rearrange("p (c d) -> p c d", c=NC)

        sf_mem = sb("sf_mem", [P, 2 * N])
        SfH = sf_mem[:, 0:N].bitcast(F16).rearrange("p (k n) -> p k n", k=H)
        SfL = sf_mem[:, N:2 * N].bitcast(F16).rearrange("p (k n) -> p k n", k=H)
        io_raw = sf_mem[:, 0:8 * D].rearrange("p (w k m) -> p w k m", w=4, k=H)

        deg_mem = sb("deg_mem", [P, 2 * N])
        Dr, Dc = deg_mem[:, 0:N], deg_mem[:, N:2 * N]
        w0_sb = deg_mem[:, 0:H * D].rearrange("p (k m) -> p k m", k=H)
        xT = deg_mem[:, H * D:H * D + 4 * D].rearrange("p (s k n) -> p s k n", s=4, k=H)
        yres = deg_mem[:, H * D + 4 * D:H * D + 6 * D].rearrange("p (s d) -> p s d", s=2)

        ps = ctx.enter_context(nc.psum_tensor("ps", [P, 8, TW], F32))

        def ps16(b):
            return ps[:, b, :].bitcast(F16)

        XG = [(0, 4), (4, 8), (8, NC)]
        x_in = [sem(f"x_in{i}") for i in range(3)]
        adj_in = [sem(f"adj_in{c}") for c in range(NC)]
        w0_in = sem("w0_in")
        gates_in = sem("gates_in")
        io_in = sem("io_in")
        bias_in = sem("bias_in")
        ones_ready = sem("ones_ready")
        id_zero = sem("id_zero")
        id_ready = sem("id_ready")
        xT_ps = sem("xT_ps")
        xT_sb = sem("xT_sb")
        y_ps = sem("y_ps")
        y_hi = sem("y_hi")
        y_rest = sem("y_rest")
        y_mid = sem("y_mid")
        y_ready = sem("y_ready")
        at_psA = sem("at_psA")
        at_psB = sem("at_psB")
        at_sbA = sem("at_sbA")
        at_sbB = sem("at_sbB")
        l0_done = sem("l0_done")
        rdeg_ready = sem("rdeg_ready")
        cdeg_ready = sem("cdeg_ready")
        norm_ready = sem("norm_ready")
        relu_ready = sem("relu_ready")
        res_ready = sem("res_ready")
        stat_ready = sem("stat_ready")
        mv_ready = sem("mv_ready")
        clip_ready = sem("clip_ready")
        eps_ready = sem("eps_ready")
        std_ready = sem("std_ready")
        rstd_ready = sem("rstd_ready")
        x1_ready = sem("x1_ready")
        prep_ps = sem("prep_ps")
        prep_sb = sem("prep_sb")
        c32_free = sem("c32_free")
        w_hi = sem("w_hi")
        w_ready = sem("w_ready")
        xb_ready = sem("xb_ready")
        agg_done = sem("agg_done")
        uv_hi = sem("uv_hi")
        uv_lo = sem("uv_lo")
        gate_done = [sem(f"{g}_done") for g in "rzh"]
        gate_sum = sem("gate_sum")
        gate_pre = [sem(f"{g}_pre") for g in "rzh"]
        gate_act = [sem(f"{g}_act") for g in "rzh"]
        rs_m = sem("rs_m")
        rs_hi = sem("rs_hi")
        rs_lo = sem("rs_lo")
        upd = sem("upd")
        s_hi = sem("s_hi")
        s_lo = sem("s_lo")
        tn_ps = sem("tn_ps")
        tn_hi = sem("tn_hi")
        tn_lo = sem("tn_lo")
        o1_done = sem("o1_done")
        tanh_ready = sem("tanh_ready")
        tm_ready = sem("tm_ready")
        t_hi = sem("t_hi")
        t_lo = sem("t_lo")
        o2_done = sem("o2_done")
        y2_ready = sem("y2_ready")
        st2_ready = sem("st2_ready")
        mv2_ready = sem("mv2_ready")
        std2_ready = sem("std2_ready")
        rstd2_ready = sem("rstd2_ready")
        out_ready = sem("out_ready")
        out_written = sem("out_written")

        PAIRS = [6, 0, 2, 4]
        JOBS = ([("gate", k) for k in range(KC)] + [("fuse", k) for k in range(4)]
                + [("vec", 0), ("outw", 0), ("deg", 0), ("deg", 1), ("deg", 2)]
                + [("state", t) for t in range(NT)])
        GATE_ORDER = [0, 1, 2, 3, 4, 5]
        SPLIT_JOBS = [j for j, (kind, k) in enumerate(JOBS)
                      if kind in ("fuse", "outw") or (kind == "gate" and GATE_ORDER[k] >= 4)]

        def pair(j):
            return PAIRS[j % 4]

        AGG = 4
        BANK = {0: (0, 2, 0), 1: (0, 2, 0), 2: (4, 6, 2)}
        TBANK = {0: 4, 1: 0, 2: 0}

        block = ctx.enter_context(nc.Block())

        @block.sync
        def _(sp):
            for g, (a, b) in enumerate(XG):
                full = min(b, NF)
                sp.dma_start(X[:, a:full, :], x[a * P:full * P, :].rearrange("(c p) d -> p c d", p=P)) \
                  .then_inc(x_in[g], 16)
                if full < b:
                    sp.dma_start(X[0:rows(full), full, :], x[full * P:N, :]).then_inc(x_in[g], 16)
                if g == 0:
                    sp.dma_start(w0_sb, w0.rearrange("(k p) m -> p k m", p=P)).then_inc(w0_in, 16)
            for q, w in enumerate((r_W, z_W, h_W)):
                sp.dma_start(gates_raw[:, q * H:(q + 1) * H, :], w.rearrange("(k p) m -> p k m", p=P)) \
                  .then_inc(gates_in, 16)
            for i, w in enumerate((in_W, out_W, o1_W, o2_W)):
                sp.dma_start(io_raw[:, i], w.rearrange("(k p) m -> p k m", p=P)).then_inc(io_in, 16)
            with nc.allow_non_contiguous_dma(reason="biases become columns, once"):
                for i, b in enumerate((in_b, out_b)):
                    sp.dma_start(b_in[:, i, :], b.rearrange("(k p) -> p k", p=P)).then_inc(bias_in, 16)
                for q, b in enumerate((r_b, z_b, h_b)):
                    sp.dma_start(b_gate[:, q * H:(q + 1) * H], b.rearrange("(k p) -> p k", p=P)) \
                      .then_inc(bias_in, 16)
                sp.dma_start(b_o1[:, :], o1_b.rearrange("(k p) -> p k", p=P)).then_inc(bias_in, 16)
            sp.dma_start(b_o2[:, :], o2_b.rearrange("(a d) -> a d", a=1).to_broadcast([P, D])).then_inc(bias_in, 16)

            writes = 0
            for t in range(NT):
                a, b = chunks(t)[0], chunks(t)[-1] + 1
                full = min(b, NF)
                sp.wait_ge(out_ready, b)
                sp.dma_start(out[a * P:full * P, :].rearrange("(c p) d -> p c d", p=P), XB[:, a:full, :]) \
                  .then_inc(out_written, 16)
                writes += 1
                if full < b:
                    sp.dma_start(out[full * P:N, :], XB[0:rows(full), full, :]).then_inc(out_written, 16)
                    writes += 1
            sp.wait_ge(out_written, 16 * writes)

        @block.gpsimd
        def _(pool):
            nc.gpsimd.memset(ident[:, :], 0.0).then_inc(id_zero, 1)
            pool.wait_ge(id_zero, 1)
            nc.gpsimd.affine_select(out=ident[:, :], in_=ident[:, :], compare_op=ALU.not_equal, fill=1.0,
                                    base=0, pattern=[[-1, P]], channel_multiplier=1).then_inc(id_ready, 1)
            for c in range(NC):
                pool.dma_start(A[0:rows(c), c, :], adj[c * P:c * P + rows(c), :]).then_inc(adj_in[c], 16)
            pool.wait_ge(id_ready, 1)
            nc.gpsimd.tensor_copy(ident16[:, :], ident[:, :]).then_inc(id_ready, 1)

            for n, j in enumerate(SPLIT_JOBS):
                kind, k = JOBS[j]
                src = c32[:, n % 2, :]
                if kind == "outw":
                    hi, lo, hp = (w[:, 0:3, :].rearrange("p a b -> p (a b)") for w in (Oh, Ol, Op))
                else:
                    kc = GATE_ORDER[k] if kind == "gate" else k
                    hi, lo, hp = Wh[:, kc, :], Wl[:, kc, :], Wp[:, kc, :]
                pool.wait_ge(prep_sb, j + 1)
                nc.gpsimd.tensor_copy(hi, src).then_inc(w_hi, 1)
                pool.wait_ge(w_hi, n + 1)
                nc.gpsimd.tensor_tensor(lo, src, hi, ALU.subtract).then_inc(c32_free, 1)
                nc.gpsimd.tensor_scalar(hp, hi, 1.0 / LO, None, ALU.mult).then_inc(w_ready, 1)
            pool.wait_ge(prep_sb, SPLIT_JOBS[-1] + 1)
            n = len(SPLIT_JOBS)
            hi, lo, hp = (w[:, 3, :] for w in (Oh, Ol, Op))
            src = c32[:, n % 2, 0:D]
            nc.gpsimd.tensor_copy(hi, src).then_inc(w_hi, 1)
            pool.wait_ge(w_hi, n + 1)
            nc.gpsimd.tensor_tensor(lo, src, hi, ALU.subtract).then_inc(c32_free, 1)
            nc.gpsimd.tensor_scalar(hp, hi, 1.0 / LO, None, ALU.mult).then_inc(w_ready, 1)

            pool.wait_ge(prep_ps, JOBS.index(("vec", 0)) + 1)
            pool.wait_ge(bias_in, 16 * 7)
            for c in range(NC):
                r = rows(c)
                pool.wait_ge(x1_ready, c + 1)
                nc.gpsimd.tensor_tensor(XB[0:r, c, :], X[0:r, c, :], b_o2[0:r, :], ALU.add) \
                  .then_inc(xb_ready, 1)

        @block.tensor
        def _(pe):
            mm = nc.tensor.matmul

            def x_transposes(c):
                r = rows(c)
                g = [i for i, (a, b) in enumerate(XG) if a <= c < b][0]
                pe.wait_ge(x_in[g], 16 * (1 + (XG[g][1] > NF)))
                if c >= 4:
                    pe.wait_ge(xT_sb, c - 3)
                for k in range(H):
                    ins = nc.tensor.transpose(ps[:, c % 4, k * P:k * P + r], X[0:r, c, k * P:(k + 1) * P],
                                              ident[0:r, 0:r])
                ins.then_inc(xT_ps, 1)

            def x_times_w0(c):
                r = rows(c)
                pe.wait_ge(xT_sb, c + 1)
                if c == 0:
                    pe.wait_ge(w0_in, 16)
                if c >= 4:
                    pe.wait_ge(y_rest, c - 3)
                for k in range(H):
                    ins = mm(ps[0:r, 4 + c % 4, 0:D], xT[:, c % 4, k, 0:r], w0_sb[:, k, :],
                             start=(k == 0), stop=(k == H - 1))
                ins.then_inc(y_ps, 1)

            pe.wait_ge(id_ready, 1)
            for c in range(NC + 2):
                if c < NC:
                    x_transposes(c)
                if c >= 2:
                    x_times_w0(c - 2)

            pe.wait_ge(id_ready, 2)
            pe.wait_ge(ones_ready, 1)
            pe.wait_ge(y_rest, NC)
            def first_layer(j):
                rj = rows(j)
                pe.wait_ge(adj_in[j], 16)
                if j == 0:
                    pe.wait_ge(y_ready, 1)
                else:
                    pe.wait_ge(y_ready, j + 1)
                for i in range(NC):
                    ri = rows(i)
                    a = A[0:rj, j, i * P:i * P + ri]
                    ins = mm(ps[0:ri, 5, D + i:D + i + 1], a, ones16[0:rj, :],
                             start=(j == 0 and i == 0), stop=(j == NC - 1), skip_group_check=True)
                    for s in range(3):
                        ins = mm(ps[0:ri, i // 2, (i % 2) * D:(i % 2 + 1) * D], a, Y[0:rj, s, j, :],
                                 start=(j == 0 and s == 0 and i % 2 == 0 and i // 2 < 5),
                                 stop=(j == NC - 1 and s == 2), skip_group_check=True)
                    if j == NC - 1:
                        ins.then_inc(l0_done, 1)

            def adj_transposes(j):
                rj = rows(j)
                if j >= 1:
                    pe.wait_ge(at_sbA, j)
                for i in range(6):
                    ins = nc.tensor.transpose(ps16(6)[:, i * P:i * P + rj], A[0:rj, j, i * P:(i + 1) * P],
                                              ident16[0:rj, 0:rj])
                ins.then_inc(at_psA, 1)
                if j >= 1:
                    pe.wait_ge(at_sbB, 2 * j)
                for i in range(6, NC):
                    ri = rows(i)
                    ins = nc.tensor.transpose(ps16(7)[0:ri, (i - 6) * P:(i - 6) * P + rj],
                                              A[0:rj, j, i * P:i * P + ri], ident16[0:rj, 0:rj])
                ins.then_inc(at_psB, 1)

            for j in range(NC):
                pe.wait_ge(adj_in[j], 16)
                adj_transposes(j)
                first_layer(j)

            pe.wait_ge(gates_in, 16 * 3)
            pe.wait_ge(io_in, 16 * 4)
            pe.wait_ge(bias_in, 16 * 7)
            pe.wait_ge(at_sbA, NC)
            pe.wait_ge(at_sbB, 2 * NC)
            for j, (kind, k) in enumerate(JOBS):
                b = pair(j)
                if 1 <= j < 4:
                    pe.wait_ge(relu_ready, min(2 * b + 4, NC))
                    if b == 4:
                        pe.wait_ge(cdeg_ready, 2)
                if j >= 4:
                    pe.wait_ge(prep_sb, j - 3)
                if kind == "gate":
                    kc = GATE_ORDER[k]
                    for m in range(M6):
                        ins = nc.tensor.transpose(ps[:, b + m // 3, (m % 3) * P:(m % 3 + 1) * P],
                                                  gates_raw[:, m, kc * P:(kc + 1) * P], ident[:, :])
                elif kind == "fuse":
                    w, kh = divmod(k, H)
                    if k == 0:
                        pe.wait_ge(prep_sb, 4)
                    for hf in range(2):
                        for m in range(H):
                            ins = mm(ps[:, b + hf, 0:G // 2], io_raw[:, w, m, kh * P:(kh + 1) * P],
                                     gT[:, w * H + m, hf * G // 2:(hf + 1) * G // 2],
                                     start=(m == 0), stop=(m == H - 1))
                elif kind == "vec":
                    first = True
                    for w in range(2):
                        for m in range(M6):
                            for kk in range(H):
                                ins = mm(ps[:, b, w * M6 + m:w * M6 + m + 1],
                                         gT[:, w * H + kk, m * P:(m + 1) * P], b_in[:, w, kk:kk + 1],
                                         start=first, stop=(kk == H - 1), skip_group_check=True)
                                first = False
                elif kind == "outw":
                    for w in range(2):
                        for kk in range(H):
                            for m in range(H):
                                ins = nc.tensor.transpose(
                                    ps[:, b + w, kk * D + m * P:kk * D + (m + 1) * P],
                                    io_raw[:, 2 + w, m, kk * P:(kk + 1) * P], ident[:, :])
                elif kind == "deg":
                    if k == 0:
                        pe.wait_ge(rdeg_ready, NC)
                    jobs = ([(rdeg, c, b + c // CPT, c % CPT) for c in range(2 * CPT)] if k == 0 else
                            [(cdeg, c, b + c // CPT, c % CPT) for c in range(2 * CPT)] if k == 1 else
                            [(d, c, b + n, c - 2 * CPT) for n, d in enumerate((rdeg, cdeg))
                             for c in range(2 * CPT, NC)])
                    for d, c, bank, at in jobs:
                        r = rows(c)
                        ins = mm(ps[:, bank, at * P:at * P + r], d[0:r, c:c + 1].to_broadcast([r, P]),
                                 ident[0:r, 0:r], start=True, stop=True)
                else:
                    for c in chunks(k):
                        r = rows(c)
                        pe.wait_ge(x1_ready, c + 1)
                        for hf in range(H):
                            ins = nc.tensor.transpose(ps[:, b + hf, (c % CPT) * P:(c % CPT) * P + r],
                                                      X[0:r, c, hf * P:(hf + 1) * P], ident[0:r, 0:r])
                ins.then_inc(prep_ps, 1)
            pe.wait_ge(prep_sb, len(JOBS))
            pe.wait_ge(w_ready, len(SPLIT_JOBS) + 1)

            def neighbours(t, ks, first, last):
                a, n = TILES[t]
                for g in range(2 * H):
                    adjacency = AT if g < H else A
                    f = (g % H) * P
                    for k in ks:
                        r = rows(k)
                        for part in (SnH, SnL):
                            ins = mm(ps[:, AGG + g, 0:n], part[0:r, k, f:f + P], adjacency[0:r, k, a:a + n],
                                     start=(first and k == ks[0] and part is SnH),
                                     stop=(last and k == ks[-1] and part is SnL))
                    if last and g % H == H - 1:
                        ins.then_inc(agg_done, 1)

            def gate_products(t, q, m, kcs, first, last):
                a, n = TILES[t]
                col = (q * H + m) * P
                for kc in kcs:
                    if kc < 2 * H:
                        hi, lo = UVH[:, kc, a:a + n], UVL[:, kc, a:a + n]
                    elif q < 2:
                        hi, lo = SfH[:, kc - 2 * H, a:a + n], SfL[:, kc - 2 * H, a:a + n]
                    else:
                        hi, lo = rsH[:, kc - 2 * H, 0:n], rsL[:, kc - 2 * H, 0:n]
                    for w, v in ((Wh, hi), (Wl, hi), (Wp, lo)):
                        ins = mm(ps[:, BANK[t][q] + m, 0:n], w[:, kc, col:col + P], v,
                                 start=(first and kc == kcs[0] and w is Wh),
                                 stop=(last and kc == kcs[-1] and w is Wp))
                return ins

            def state_transposes(t, hi_ready, lo_ready):
                for i, (part, ready) in enumerate(((SfH, hi_ready), (SfL, lo_ready))):
                    pe.wait_ge(*ready)
                    for c in chunks(t):
                        r = rows(c)
                        for hf in range(H):
                            at = (c % CPT) * D + hf * P
                            ins = nc.tensor.transpose(ps16(TBANK[t] + i)[0:r, at:at + P],
                                                      part[:, hf, c * P:c * P + r], ident16[:, :])
                    ins.then_inc(tn_ps, 1)

            def gates(t, st, before_rs=None):
                for q in range(2):
                    for m in range(H):
                        ins = gate_products(t, q, m, range(KC), True, True)
                    ins.then_inc(gate_done[q], 1)
                if t < 2:
                    pe.wait_ge(gate_pre[0], 2 * NT * st + 2 * t + 2)
                else:
                    pe.wait_ge(gate_pre[1], 2 * NT * st + 2 * t)
                for m in range(H):
                    gate_products(t, 2, m, range(2 * H), True, False)
                if before_rs:
                    before_rs()
                pe.wait_ge(rs_hi, NT * st + t + 1)
                pe.wait_ge(rs_lo, NT * st + t + 1)
                for m in range(H):
                    ins = gate_products(t, 2, m, range(2 * H, KC), False, True)
                ins.then_inc(gate_done[2], 1)

            with pe.Fori(0, STEPS) as st:
                pe.wait_ge(tn_hi, 4 * st + 2)
                pe.wait_ge(tn_lo, 4 * st + 2)
                neighbours(0, range(0, 2 * CPT), True, False)
                state_transposes(2, (s_hi, NT * st + 3), (s_lo, NT * st + 3))
                pe.wait_ge(tn_hi, 4 * st + 4)
                pe.wait_ge(tn_lo, 4 * st + 4)
                neighbours(0, range(2 * CPT, NC), False, True)
                for t in (1, 2):
                    pe.wait_ge(uv_hi, 6 * st + 2 * t)
                    pe.wait_ge(uv_lo, 6 * st + 2 * t)
                    neighbours(t, range(NC), True, True)
                    if t == 1:
                        gates(0, st)
                pe.wait_ge(uv_hi, 6 * st + 6)
                pe.wait_ge(uv_lo, 6 * st + 6)
                state_transposes(0, (s_hi, NT * st + 4), (s_lo, NT * st + 4))
                gates(1, st)
                pe.wait_ge(tn_hi, 4 * st + 5)
                pe.wait_ge(tn_lo, 4 * st + 5)
                gates(2, st, lambda: state_transposes(1, (s_hi, NT * st + 5), (s_lo, NT * st + 5)))

            O1_BANK = (0, 4, 6)
            O2_BANK = (2, 0, 4)

            def out1(t):
                a, n = TILES[t]
                for m in range(H):
                    for kk in range(H):
                        for w, v in ((Oh, SfH), (Ol, SfH), (Op, SfL)):
                            ins = mm(ps[:, O1_BANK[t] + m, 0:n], w[:, kk, m * P:(m + 1) * P],
                                     v[:, kk, a:a + n], start=(kk == 0 and w is Oh),
                                     stop=(kk == H - 1 and w is Op))
                ins.then_inc(o1_done, 1)

            def out2(t):
                pe.wait_ge(t_hi, t + 1)
                pe.wait_ge(t_lo, t + 1)
                for c in chunks(t):
                    r = rows(c)
                    bank, at = O2_BANK[t] + (c % CPT) // 2, (c % 2) * D
                    for kk in range(H):
                        for v, w in ((TH, Oh), (TH, Ol), (TL, Op)):
                            ins = mm(ps[0:r, bank, at:at + D], v[:, kk, c * P:c * P + r], w[:, H + kk, :],
                                     start=(kk == 0 and w is Oh), stop=(kk == H - 1 and w is Op))
                    ins.then_inc(o2_done, 1)

            pe.wait_ge(tn_hi, 4 * STEPS + 2)
            pe.wait_ge(tn_lo, 4 * STEPS + 2)
            out1(0)
            out1(1)
            pe.wait_ge(s_hi, NT * STEPS + 3)
            pe.wait_ge(s_lo, NT * STEPS + 3)
            out1(2)
            out2(0)
            pe.wait_ge(tanh_ready, 4)
            out2(1)
            out2(2)

        @block.scalar
        def _(act):
            def copy(o, i, scale=1.0):
                return nc.scalar.activation(o, i, ACT.Copy, scale=scale)

            for c in range(NC + 2):
                if c < NC:
                    r = rows(c)
                    act.wait_ge(xT_ps, c + 1)
                    if c >= 4:
                        act.wait_ge(y_ps, c - 3)
                    copy(xT[:, c % 4, :, 0:r],
                         ps[:, c % 4, 0:D].rearrange("p (k n) -> p k n", k=H)[:, :, 0:r]).then_inc(xT_sb, 1)
                if c >= 2:
                    e = c - 2
                    r = rows(e)
                    act.wait_ge(y_ps, e + 1)
                    copy(Y[0:r, 0, e, :], ps[0:r, 4 + e % 4, 0:D]).then_inc(y_hi, 1)
                    act.wait_ge(y_rest, e + 1)
                    copy(Y[0:r, 1, e, :], yres[0:r, e % 2, :]).then_inc(y_mid, 1)

            for j in range(NC):
                rj = rows(j)
                act.wait_ge(at_psA, j + 1)
                copy(AT[:, 0:6, j * P:j * P + rj],
                     ps16(6)[:, 0:6 * P].rearrange("p (i n) -> p i n", i=6)[:, :, 0:rj]).then_inc(at_sbA, 1)

            def roots(t, mv_done, done):
                for r, c0, c1 in column_runs(t):
                    act.wait_ge(mv_done, c1)
                    nc.scalar.activation(rstd[0:r, c0:c1], mv[0:r, c0:c1, 1], ACT.Sqrt, bias=eps[0:r, :]) \
                        .then_inc(done, 1)

            act.wait_ge(clip_ready, 4)
            act.wait_ge(eps_ready, 1)
            for r, c0, c1 in ((P, 0, NF), (rows(NF), NF, NC)):
                nc.scalar.activation(norm[0:r, c0:c1], norm[0:r, c0:c1], ACT.Sqrt).then_inc(norm_ready, 1)
            act.wait_ge(norm_ready, 2)
            for c in range(NC):
                r = rows(c)
                act.wait_ge(l0_done, c + 1)
                if c >= 4:
                    act.wait_ge(res_ready, c - 3)
                nc.scalar.activation(relu[0:r, c % 4, :], ps[0:r, c // 2, (c % 2) * D:(c % 2 + 1) * D],
                                     ACT.Relu, scale=norm[0:r, c:c + 1]).then_inc(relu_ready, 1)
                if c == 2 * CPT - 1:
                    roots(0, mv_ready, std_ready)
            roots(1, mv_ready, std_ready)

            split = 0
            for j, (kind, k) in enumerate(JOBS):
                b = pair(j)
                three = ps[:, b:b + 2, 0:G // 2]
                act.wait_ge(prep_ps, j + 1)
                if j == 2:
                    roots(2, mv_ready, std_ready)
                if j in SPLIT_JOBS and split >= 2 and kind != "outw":
                    act.wait_ge(c32_free, split - 1)
                if kind == "gate" and GATE_ORDER[k] < 4:
                    ins = copy(gT[:, GATE_ORDER[k], :].rearrange("p (a g) -> p a g", a=2), three)
                elif kind in ("gate", "fuse"):
                    ins = copy(c32[:, split % 2, :].rearrange("p (a g) -> p a g", a=2), three, WS)
                    split += 1
                elif kind == "vec":
                    ins = copy(v_gate[:, :, :].rearrange("p w m -> p (w m)"), ps[:, b, 0:2 * M6], WS)
                elif kind == "outw":
                    act.wait_ge(c32_free, split)
                    both = ps[:, b:b + 2, :].rearrange("p a b -> p (a b)")
                    copy(c32[:, split % 2, :], both[:, 0:3 * D], WS)
                    ins = copy(c32[:, (split + 1) % 2, 0:D], both[:, 3 * D:4 * D], WS)
                elif kind == "deg":
                    if k < 2:
                        ins = copy((Dr, Dc)[k][:, 0:2 * TW].rearrange("p (a n) -> p a n", a=2), ps[:, b:b + 2, :])
                    else:
                        n = N - 2 * TW
                        copy(Dr[:, 2 * TW:N], ps[:, b, 0:n])
                        ins = copy(Dc[:, 2 * TW:N], ps[:, b + 1, 0:n])
                else:
                    a, n = TILES[k]
                    copy(SfH[:, :, a:a + n], ps[:, b:b + 2, 0:n]).then_inc(s_hi, 1)
                    if k < 2:
                        cs = chunks(k)
                        copy(SnH[:, cs[0]:cs[-1] + 1, :], X[:, cs[0]:cs[-1] + 1, :], LO).then_inc(tn_hi, 1)
                    ins = copy(Sm[:, :, a:a + n], ps[:, b:b + 2, 0:n], LO)
                ins.then_inc(prep_sb, 1)

            def neighbours_hi(t, st):
                a, n = TILES[t]
                for s in range(2):
                    act.wait_ge(agg_done, 6 * st + 2 * t + s + 1)
                    copy(UVH[:, s * H:(s + 1) * H, a:a + n], ps[:, AGG + s * H:AGG + (s + 1) * H, 0:n], 1 / LO) \
                        .then_inc(uv_hi, 1)

            def gate(t, st, q, buf, func):
                a, n = TILES[t]
                for m in range(H):
                    act.wait_ge(gate_pre[q], 2 * NT * st + 2 * t + m + 1)
                    nc.scalar.activation(buf[:, m, 0:n], buf[:, m, 0:n], func, scale=1 / WS,
                                         bias=b_gate[:, q * H + m:q * H + m + 1]).then_inc(gate_act[q], 1)

            def gates(t, st, before_h=None):
                a, n = TILES[t]
                gate(t, st, 0, gR, ACT.Sigmoid)
                act.wait_ge(rs_m, NT * st + t + 1)
                copy(rsH[:, :, 0:n], gR[:, :, 0:n], 1 / LO).then_inc(rs_hi, 1)
                gate(t, st, 1, gZ, ACT.Sigmoid)
                if before_h:
                    before_h()
                gate(t, st, 2, gH, ACT.Tanh)
                act.wait_ge(upd, 3 * NT * st + 3 * t + 3)
                copy(SfH[:, :, a:a + n], Sm[:, :, a:a + n], 1 / LO).then_inc(s_hi, 1)

            def state_nodes(t, count):
                act.wait_ge(tn_ps, count)
                c0, full = chunks(t)[0], min(chunks(t)[-1] + 1, NF)
                nf = full - c0
                copy(SnH[:, c0:full, :], ps16(TBANK[t])[:, 0:nf * D].rearrange("p (c d) -> p c d", c=nf), LO) \
                    .then_inc(tn_hi, 1)
                if full <= chunks(t)[-1]:
                    r = rows(full)
                    copy(SnH[0:r, full, :], ps16(TBANK[t])[0:r, nf * D:(nf + 1) * D], LO).then_inc(tn_hi, 1)

            with act.Fori(0, STEPS) as st:
                state_nodes(2, 6 * st + 1)
                neighbours_hi(0, st)
                neighbours_hi(1, st)
                gates(0, st)
                neighbours_hi(2, st)
                state_nodes(0, 6 * st + 3)
                gates(1, st)
                gates(2, st, lambda: state_nodes(1, 6 * st + 5))

            for t in range(NT):
                a, n = TILES[t]
                act.wait_ge(o1_done, t + 1)
                for m in range(H):
                    nc.scalar.activation(Tm[:, m, a:a + n], ps[:, (0, 4, 6)[t] + m, 0:n], ACT.Tanh,
                                         scale=1 / WS, bias=b_o1[:, m:m + 1]).then_inc(tanh_ready, 1)
                act.wait_ge(tm_ready, t + 1)
                copy(TH[:, :, a:a + n], Tm[:, :, a:a + n], 1 / LO).then_inc(t_hi, 1)
            for t in range(NT):
                roots(t, mv2_ready, std2_ready)

        @block.vector
        def _(dve):
            nc.vector.memset(ones16[:, :], 1.0).then_inc(ones_ready, 1)
            nc.vector.memset(eps[:, :], EPS).then_inc(eps_ready, 1)

            def low(o, hi, full):
                return nc.vector.scalar_tensor_tensor(out=o, in0=hi, scalar=-LO, in1=full,
                                                      op0=ALU.mult, op1=ALU.add)

            for c in range(NC):
                r = rows(c)
                dve.wait_ge(y_hi, c + 1)
                if c >= 2:
                    dve.wait_ge(y_ready, c - 1)
                nc.vector.tensor_tensor(yres[0:r, c % 2, :], ps[0:r, 4 + c % 4, 0:D], Y[0:r, 0, c, :],
                                        ALU.subtract).then_inc(y_rest, 1)
                dve.wait_ge(y_mid, c + 1)
                nc.vector.tensor_tensor(Y[0:r, 2, c, :], yres[0:r, c % 2, :], Y[0:r, 1, c, :],
                                        ALU.subtract).then_inc(y_ready, 1)

            for j in range(NC):
                rj = rows(j)
                dve.wait_ge(at_psB, j + 1)
                four = ps16(7)[:, 0:(NF - 6) * P].rearrange("p (i n) -> p i n", i=NF - 6)
                nc.vector.tensor_copy(AT[:, 6:NF, j * P:j * P + rj], four[:, :, 0:rj]).then_inc(at_sbB, 1)
                rl = rows(NF)
                nc.vector.tensor_copy(AT[0:rl, NF, j * P:j * P + rj],
                                      ps16(7)[0:rl, (NF - 6) * P:(NF - 6) * P + rj]).then_inc(at_sbB, 1)
                nc.vector.tensor_reduce(rdeg[0:rj, j:j + 1], A[0:rj, j, :], AX_X, ALU.add).then_inc(rdeg_ready, 1)

            dve.wait_ge(l0_done, NC)
            rl = rows(NF)
            for r, a, b in ((P, 0, NF), (rl, NF, NC)):
                nc.vector.tensor_copy(cdeg[0:r, a:b], ps[0:r, 5, D + a:D + b]).then_inc(cdeg_ready, 1)
            dve.wait_ge(cdeg_ready, 2)
            for r, a, b in ((P, 0, NF), (rl, NF, NC)):
                nc.vector.tensor_scalar(norm[0:r, a:b], cdeg[0:r, a:b], 1.0, None, ALU.max).then_inc(clip_ready, 1)
            dve.wait_ge(clip_ready, 2)
            for r, a, b in ((P, 0, NF), (rl, NF, NC)):
                nc.vector.reciprocal(norm[0:r, a:b], norm[0:r, a:b]).then_inc(clip_ready, 1)

            def layer_norm(t, src, dst, sems):
                s_stat, s_mv, s_std, s_rstd, s_out = sems
                cs = chunks(t)
                for c in cs:
                    nc.vector.bn_stats(stats[0:rows(c), c, :], src[0:rows(c), c, :]).then_inc(s_stat, 1)
                for c in cs:
                    dve.wait_ge(s_stat, c + 1)
                    nc.vector.bn_aggr(mv[0:rows(c), c, :], stats[0:rows(c), c, :]).then_inc(s_mv, 1)
                for r, c0, c1 in column_runs(t):
                    dve.wait_ge(s_std, t + 1 + (c1 > NF))
                    nc.vector.reciprocal(rstd[0:r, c0:c1], rstd[0:r, c0:c1]).then_inc(s_rstd, 1)
                for c in cs:
                    r = rows(c)
                    dve.wait_ge(s_rstd, t + 1 + (c >= NF))
                    nc.vector.tensor_scalar(dst[0:r, c, :], src[0:r, c, :], mv[0:r, c, 0:1], rstd[0:r, c:c + 1],
                                            ALU.subtract, ALU.mult).then_inc(s_out, 1)

            for t in range(NT):
                for c in chunks(t):
                    r = rows(c)
                    dve.wait_ge(relu_ready, c + 1)
                    nc.vector.tensor_tensor(X[0:r, c, :], X[0:r, c, :], relu[0:r, c % 4, :], ALU.add) \
                        .then_inc(res_ready, 1)
                dve.wait_ge(res_ready, chunks(t)[-1] + 1)
                layer_norm(t, X, X, (stat_ready, mv_ready, std_ready, rstd_ready, x1_ready))

            for t in range(NT):
                a, n = TILES[t]
                dve.wait_ge(prep_sb, JOBS.index(("state", t)) + 1)
                dve.wait_ge(s_hi, t + 1)
                low(SfL[:, :, a:a + n], SfH[:, :, a:a + n], Sm[:, :, a:a + n]).then_inc(s_lo, 1)
                if t < 2:
                    dve.wait_ge(tn_hi, t + 1)
                    c0, c1 = chunks(t)[0], chunks(t)[-1] + 1
                    nc.vector.scalar_tensor_tensor(
                        out=SnL[:, c0:c1, :], in0=X[:, c0:c1, :], scalar=LO, in1=SnH[:, c0:c1, :],
                        op0=ALU.mult, op1=ALU.subtract).then_inc(tn_lo, 1)

            def neighbours_lo(t, st):
                a, n = TILES[t]
                for s in range(2):
                    dve.wait_ge(uv_hi, 6 * st + 2 * t + s + 1)
                    low(UVL[:, s * H:(s + 1) * H, a:a + n], UVH[:, s * H:(s + 1) * H, a:a + n],
                        ps[:, AGG + s * H:AGG + (s + 1) * H, 0:n]).then_inc(uv_lo, 1)

            def gate(t, st, q, buf):
                a, n = TILES[t]
                dve.wait_ge(gate_done[q], NT * st + t + 1)
                for m in range(H):
                    nc.vector.scalar_tensor_tensor(
                        out=buf[:, m, 0:n], in0=Dr[:, a:a + n], scalar=v_gate[:, 0, q * H + m:q * H + m + 1],
                        in1=ps[:, BANK[t][q] + m, 0:n], op0=ALU.mult, op1=ALU.add).then_inc(gate_sum, 1)
                for m in range(H):
                    dve.wait_ge(gate_sum, 6 * NT * st + 6 * t + 2 * q + m + 1)
                    nc.vector.scalar_tensor_tensor(
                        out=buf[:, m, 0:n], in0=Dc[:, a:a + n], scalar=v_gate[:, 1, q * H + m:q * H + m + 1],
                        in1=buf[:, m, 0:n], op0=ALU.mult, op1=ALU.add).then_inc(gate_pre[q], 1)

            def gates(t, st, before_h=None):
                a, n = TILES[t]
                gate(t, st, 0, gR)
                dve.wait_ge(gate_act[0], 2 * NT * st + 2 * t + 2)
                nc.vector.tensor_tensor(gR[:, :, 0:n], gR[:, :, 0:n], Sm[:, :, a:a + n], ALU.mult) \
                    .then_inc(rs_m, 1)
                dve.wait_ge(rs_hi, NT * st + t + 1)
                low(rsL[:, :, 0:n], rsH[:, :, 0:n], gR[:, :, 0:n]).then_inc(rs_lo, 1)
                gate(t, st, 1, gZ)
                if before_h:
                    before_h()
                gate(t, st, 2, gH)
                dve.wait_ge(gate_act[2], 2 * NT * st + 2 * t + 2)
                nc.vector.scalar_tensor_tensor(out=gH[:, :, 0:n], in0=gH[:, :, 0:n], scalar=LO,
                                               in1=Sm[:, :, a:a + n], op0=ALU.mult,
                                               op1=ALU.subtract).then_inc(upd, 1)
                dve.wait_ge(gate_act[1], 2 * NT * st + 2 * t + 2)
                dve.wait_ge(upd, 3 * NT * st + 3 * t + 1)
                nc.vector.tensor_tensor(gH[:, :, 0:n], gH[:, :, 0:n], gZ[:, :, 0:n], ALU.mult).then_inc(upd, 1)
                dve.wait_ge(upd, 3 * NT * st + 3 * t + 2)
                nc.vector.tensor_tensor(Sm[:, :, a:a + n], Sm[:, :, a:a + n], gH[:, :, 0:n], ALU.add) \
                    .then_inc(upd, 1)
                dve.wait_ge(s_hi, NT * st + 3 + t + 1)
                low(SfL[:, :, a:a + n], SfH[:, :, a:a + n], Sm[:, :, a:a + n]).then_inc(s_lo, 1)

            def state_nodes(t, count):
                dve.wait_ge(tn_ps, count)
                c0, full = chunks(t)[0], min(chunks(t)[-1] + 1, NF)
                nf = full - c0
                b = ps16(TBANK[t] + 1)
                nc.vector.tensor_copy(SnL[:, c0:full, :], b[:, 0:nf * D].rearrange("p (c d) -> p c d", c=nf)) \
                    .then_inc(tn_lo, 1)
                if full <= chunks(t)[-1]:
                    r = rows(full)
                    nc.vector.tensor_copy(SnL[0:r, full, :], b[0:r, nf * D:(nf + 1) * D]).then_inc(tn_lo, 1)

            dve.wait_ge(prep_sb, len(JOBS))
            with dve.Fori(0, STEPS) as st:
                state_nodes(2, 6 * st + 2)
                neighbours_lo(0, st)
                neighbours_lo(1, st)
                gates(0, st)
                neighbours_lo(2, st)
                state_nodes(0, 6 * st + 4)
                gates(1, st)
                gates(2, st, lambda: state_nodes(1, 6 * st + 6))

            def split_tanh(t):
                a, n = TILES[t]
                dve.wait_ge(tanh_ready, 2 * t + 2)
                nc.vector.tensor_scalar(Tm[:, :, a:a + n], Tm[:, :, a:a + n], LO, None, ALU.mult) \
                    .then_inc(tm_ready, 1)
                dve.wait_ge(t_hi, t + 1)
                low(TL[:, :, a:a + n], TH[:, :, a:a + n], Tm[:, :, a:a + n]).then_inc(t_lo, 1)

            def last_norm(t):
                for c in chunks(t):
                    r = rows(c)
                    bank, at = (2, 0, 4)[t] + (c % CPT) // 2, (c % 2) * D
                    dve.wait_ge(o2_done, min(c // 2 * 2 + 2, NC))
                    dve.wait_ge(xb_ready, c + 1)
                    nc.vector.scalar_tensor_tensor(out=XB[0:r, c, :], in0=ps[0:r, bank, at:at + D], scalar=1 / WS,
                                                   in1=XB[0:r, c, :], op0=ALU.mult, op1=ALU.add) \
                        .then_inc(y2_ready, 1)
                dve.wait_ge(y2_ready, chunks(t)[-1] + 1)
                layer_norm(t, XB, XB, (st2_ready, mv2_ready, std2_ready, rstd2_ready, out_ready))

            for t in range(NT):
                split_tanh(t)
            for t in range(NT):
                last_norm(t)


_INS = ['x', 'adj', 'L0_gnn_weight', 'L1_gnn_in_W', 'L1_gnn_in_b', 'L1_gnn_out_W', 'L1_gnn_out_b',
        'L1_gnn_r_W', 'L1_gnn_r_b', 'L1_gnn_z_W', 'L1_gnn_z_b', 'L1_gnn_h_W', 'L1_gnn_h_b',
        'L1_gnn_o1_W', 'L1_gnn_o1_b', 'L1_gnn_o2_W', 'L1_gnn_o2_b']


def kernel(**inputs):
    import numpy as _np
    import concourse.bacc as _bacc
    from concourse import mybir as _mybir
    from concourse.bass_utils import run_bass_kernel_spmd as _run

    nc = _bacc.Bacc("TRN2", target_bir_lowering=False, num_devices=1)
    arrays, args = {}, []
    for name in _INS:
        a = _np.ascontiguousarray(inputs[name])
        arrays[f"in_{name}_dram"] = a
        args.append(nc.dram_tensor(f"in_{name}_dram", a.shape, _mybir.dt.from_np(a.dtype),
                                   kind="ExternalInput").ap())
    shape = _np.asarray(inputs['x']).shape
    args.append(nc.dram_tensor("out_0_dram", shape, _mybir.dt.float32, kind="ExternalOutput").ap())
    gated_graph_net(nc, *args)
    r = _run(nc, [arrays], core_ids=[0])
    return r.results[0]["out_0_dram"]
```

```python
from contextlib import ExitStack

import concourse.bass as bass
from concourse import mybir

ALU = mybir.AluOpType
ACT = mybir.ActivationFunctionType
AX_X = mybir.AxisListType.X
AX_XY = mybir.AxisListType.XY
F32 = mybir.dt.float32
F16 = mybir.dt.float16
I32 = mybir.dt.int32

P = 128
STEPS = 5
EPS = 1e-5
LO = 2048.0
TOP = 2.0 ** 14
LEAST = 2.0 ** -60
EXPONENT = 0x7F800000


def gated_graph_net(nc: bass.Bass, x, adj, w0, in_W, in_b, out_W, out_b, r_W, r_b, z_W, z_b,
                    h_W, h_b, o1_W, o1_b, o2_W, o2_b, out):
    N, D = x.shape
    NC = -(-N // P)
    NF = N // P
    H = D // P
    TW = 512
    TILES = [(a, min(TW, N - a)) for a in range(0, N, TW)]
    NT = len(TILES)
    CPT = TW // P
    KC = 3 * H
    M6 = 3 * H
    G = M6 * P
    assert H == 2 and NT == 3 and r_W.shape == (D, 3 * D)

    def rows(c):
        return min(P, N - c * P)

    def chunks(t):
        return range(t * CPT, min((t + 1) * CPT, NC))

    def column_runs(t):
        c0, c1 = chunks(t)[0], chunks(t)[-1] + 1
        return [(P, c0, min(c1, NF))] + ([(rows(NF), NF, c1)] if c1 > NF else [])

    with ExitStack() as ctx:
        def sb(name, shape, dt=F32):
            return ctx.enter_context(nc.sbuf_tensor(name, shape, dt))

        def sem(name):
            return ctx.enter_context(nc.semaphore(name))

        A = sb("A", [P, NC, N], F16)
        AT = sb("AT", [P, NC, N], F16)
        X = sb("X", [P, NC, D])
        SnH = sb("SnH", [P, NC, D], F16)
        SnL = sb("SnL", [P, NC, D], F16)
        Sm = sb("Sm", [P, H, N])
        Wh = sb("Wh", [P, KC, G], F16)
        Wl = sb("Wl", [P, KC, G], F16)
        Wp = sb("Wp", [P, KC, G], F16)
        Oh = sb("Oh", [P, 2 * H, D], F16)
        Ol = sb("Ol", [P, 2 * H, D], F16)
        Op = sb("Op", [P, 2 * H, D], F16)
        ident = sb("ident", [P, P])
        ident16 = sb("ident16", [P, P], F16)
        ones16 = sb("ones16", [P, 1], F16)
        b_gate = sb("b_gate", [P, M6])
        b_o1 = sb("b_o1", [P, H])
        b_o2 = sb("b_o2", [P, D])
        v_gate = sb("v_gate", [P, 2, M6])
        rdeg = sb("rdeg", [P, NC])
        cdeg = sb("cdeg", [P, NC])
        norm = sb("norm", [P, NC])
        stats = sb("stats", [P, NC, 6])
        mv = sb("mv", [P, NC, 2])
        rstd = sb("rstd", [P, NC])
        newton = sb("newton", [P, 2, NC])
        peak = sb("peak", [P, 10])
        peak_all = sb("peak_all", [P, 10])
        junk = sb("junk", [P, D])
        xscale = sb("xscale", [P, 2])
        wscale = sb("wscale", [P, 2])

        uv = sb("uv", [P, 4 * N])
        UVH = uv[:, 0:2 * N].bitcast(F16).rearrange("p (k n) -> p k n", k=2 * H)
        UVL = uv[:, 2 * N:4 * N].bitcast(F16).rearrange("p (k n) -> p k n", k=2 * H)
        gates_raw = uv[:, 0:3 * H * 3 * D].rearrange("p (k m) -> p k m", k=3 * H)
        Tm = uv[:, 0:2 * N].rearrange("p (k n) -> p k n", k=H)
        TH = uv[:, 2 * N:3 * N].bitcast(F16).rearrange("p (k n) -> p k n", k=H)
        TL = uv[:, 3 * N:4 * N].bitcast(F16).rearrange("p (k n) -> p k n", k=H)

        act_mem = sb("act_mem", [P, 4 * H * TW])
        gR, gZ, gH = (act_mem[:, q * H * TW:(q + 1) * H * TW].rearrange("p (k n) -> p k n", k=H)
                      for q in range(3))
        rs_mem = act_mem[:, 3 * H * TW:4 * H * TW].bitcast(F16).rearrange("p (s k n) -> p s k n", s=2, k=H)
        rsH, rsL = rs_mem[:, 0], rs_mem[:, 1]
        relu = act_mem[:, 0:NC * D].rearrange("p (c d) -> p c d", c=NC)
        XHL = act_mem[:, 0:NC * D].bitcast(F16).rearrange("p (s c d) -> p s c d", s=2, c=NC)

        gt_mem = sb("gt_mem", [P, 4 * G])
        gT = gt_mem[:, :].rearrange("p (k g) -> p k g", k=4)
        XB = gt_mem[:, 0:NC * D].rearrange("p (c d) -> p c d", c=NC)

        sf_mem = sb("sf_mem", [P, 2 * N])
        SfH = sf_mem[:, 0:N].bitcast(F16).rearrange("p (k n) -> p k n", k=H)
        SfL = sf_mem[:, N:2 * N].bitcast(F16).rearrange("p (k n) -> p k n", k=H)
        w0_sb = sf_mem[:, 0:2 * D].rearrange("p (k m) -> p k m", k=H)

        b_in = SnL[:, :, :].rearrange("p c d -> p (c d)")[:, 0:4 * D].bitcast(F32) \
            .rearrange("p (w d) -> p w d", w=2)
        Dr = sb("Dr", [P, N])
        Dc = sb("Dc", [P, N])
        io_W = act_mem[:, NC * D:NC * D + 4 * D].rearrange("p (w k m) -> p w k m", w=2, k=H)
        o_W = Dc[:, 0:4 * D].rearrange("p (w k m) -> p w k m", w=2, k=H)
        deg_rows = nc.dram_tensor("deg_rows", [2, N], F32).ap()

        ps = ctx.enter_context(nc.psum_tensor("ps", [P, 8, TW], F32))

        def ps16(b):
            return ps[:, b, :].bitcast(F16)

        XG = [(0, 4), (4, 8), (8, NC)]
        x_in = [sem(f"x_in{i}") for i in range(3)]
        adj_in = [sem(f"adj_in{c}") for c in range(NC)]
        w0_in = sem("w0_in")
        gates_in = sem("gates_in")
        io_in = sem("io_in")
        bias_in = sem("bias_in")
        ones_ready = sem("ones_ready")
        id_zero = sem("id_zero")
        id_ready = sem("id_ready")
        id16_ready = sem("id16_ready")
        x_peak = sem("x_peak")
        x_peak_all = sem("x_peak_all")
        x_scale = sem("x_scale")
        w_peak = sem("w_peak")
        w_peak_all = sem("w_peak_all")
        w_scale = sem("w_scale")
        v_sum = sem("v_sum")
        v_ready = sem("v_ready")
        x_hi = sem("x_hi")
        x_lo = sem("x_lo")
        at_psA = sem("at_psA")
        at_psB = sem("at_psB")
        at_sbA = sem("at_sbA")
        at_sbB = sem("at_sbB")
        gate_ps = sem("gate_ps")
        gate_T = sem("gate_T")
        sum_done = sem("sum_done")
        sum_act = sem("sum_act")
        sum_dve = sem("sum_dve")
        l0_done = sem("l0_done")
        rdeg_ready = sem("rdeg_ready")
        cdeg_ready = sem("cdeg_ready")
        norm_ready = sem("norm_ready")
        relu_ready = sem("relu_ready")
        res_ready = sem("res_ready")
        stat_ready = sem("stat_ready")
        agg_ready = sem("agg_ready")
        agg2_ready = sem("agg2_ready")
        norm_exact = sem("norm_exact")
        x_peak_part = sem("x_peak_part")
        w_max = sem("w_max")
        mv_ready = sem("mv_ready")
        clip_ready = sem("clip_ready")
        norm_root = sem("norm_root")
        std_ready = sem("std_ready")
        rstd_ready = sem("rstd_ready")
        x1_ready = sem("x1_ready")
        job_ps = sem("job_ps")
        w_hi = sem("w_hi")
        w_lo = sem("w_lo")
        w_p = sem("w_p")
        sm_ready = sem("sm_ready")
        deg_out = sem("deg_out")
        deg_in = sem("deg_in")
        nw_step = sem("nw_step")
        xb_ready = sem("xb_ready")
        agg_done = sem("agg_done")
        uv_hi = sem("uv_hi")
        uv_lo = sem("uv_lo")
        gate_done = [sem(f"{g}_done") for g in "rzh"]
        gate_sum = sem("gate_sum")
        gate_pre = [sem(f"{g}_pre") for g in "rzh"]
        gate_act = [sem(f"{g}_act") for g in "rzh"]
        rs_m = sem("rs_m")
        rs_hi = sem("rs_hi")
        rs_lo = sem("rs_lo")
        upd = sem("upd")
        s_hi = sem("s_hi")
        s_lo = sem("s_lo")
        tn_ps = sem("tn_ps")
        tn_hi = sem("tn_hi")
        tn_lo = sem("tn_lo")
        o1_done = sem("o1_done")
        tanh_ready = sem("tanh_ready")
        tm_ready = sem("tm_ready")
        t_hi = sem("t_hi")
        t_lo = sem("t_lo")
        o2_done = sem("o2_done")
        y2_ready = sem("y2_ready")
        st2_ready = sem("st2_ready")
        mv2_ready = sem("mv2_ready")
        std2_ready = sem("std2_ready")
        rstd2_ready = sem("rstd2_ready")
        out_ready = sem("out_ready")
        out_written = sem("out_written")

        CDEG_BANK, CDEG_AT = 4, N - 2 * TW
        L0_BANK = [(6 + c) % 8 for c in range(NC)]
        JOBS = [("outw", 0), ("fuse", 0), ("state", 0), ("fuse", 1), ("state", 1), ("fuse", 2),
                ("state", 2), ("fuse", 3)]
        PAIRS = [2, 4, 6, 0]
        L0_READ = [6, 8, 10, NC]

        def x_parts(c):
            g = [i for i, (a, b) in enumerate(XG) if a <= c < b][0]
            return g + 1 + (XG[g][1] > NF)

        def split_count(job):
            return 2 + [j for j in JOBS if j[0] != "state"].index(job) + 1

        AGG = 4
        BANK = {0: (0, 2, 0), 1: (0, 2, 0), 2: (4, 6, 2)}
        TBANK = {0: 4, 1: 0, 2: 0}

        block = ctx.enter_context(nc.Block())

        @block.sync
        def _(sp):
            for g, (a, b) in enumerate(XG):
                full = min(b, NF)
                sp.dma_start(X[:, a:full, :], x[a * P:full * P, :].rearrange("(c p) d -> p c d", p=P)) \
                  .then_inc(x_in[g], 16)
                if full < b:
                    sp.dma_start(X[0:rows(full), full, :], x[full * P:N, :]).then_inc(x_in[g], 16)
                if g == 2:
                    sp.dma_start(w0_sb[:, :, :], w0.rearrange("(k p) m -> p k m", p=P)).then_inc(w0_in, 16)
            for q, w in enumerate((r_W, z_W, h_W)):
                sp.dma_start(gates_raw[:, q * H:(q + 1) * H, :], w.rearrange("(k p) m -> p k m", p=P)) \
                  .then_inc(gates_in, 16)
            for place, w in ((io_W[:, 0], in_W), (io_W[:, 1], out_W), (o_W[:, 0], o1_W), (o_W[:, 1], o2_W)):
                sp.dma_start(place, w.rearrange("(k p) m -> p k m", p=P)).then_inc(io_in, 16)

            sp.wait_ge(rdeg_ready, NC)
            sp.wait_ge(cdeg_ready, 2)
            with nc.allow_non_contiguous_dma(reason="columns become rows, once"):
                for i, d in enumerate((rdeg, cdeg)):
                    sp.dma_start(deg_rows[i, 0:NF * P].rearrange("(c p) -> p c", p=P), d[:, 0:NF]) \
                      .then_inc(deg_out, 16)
                    sp.dma_start(deg_rows[i, NF * P:N].rearrange("(c p) -> p c", c=1), d[0:rows(NF), NF:NC]) \
                      .then_inc(deg_out, 16)
            sp.wait_ge(deg_out, 64)
            sp.dma_start(Dr[:, :], deg_rows[0:1, :].to_broadcast([P, N])).then_inc(deg_in, 16)
            sp.wait_ge(job_ps, JOBS.index(("outw", 0)) + 1)
            sp.dma_start(Dc[:, :], deg_rows[1:2, :].to_broadcast([P, N])).then_inc(deg_in, 16)

            writes = 0
            for t in range(NT):
                a, b = chunks(t)[0], chunks(t)[-1] + 1
                full = min(b, NF)
                sp.wait_ge(out_ready, b)
                sp.dma_start(out[a * P:full * P, :].rearrange("(c p) d -> p c d", p=P), XB[:, a:full, :]) \
                  .then_inc(out_written, 16)
                writes += 1
                if full < b:
                    sp.dma_start(out[full * P:N, :], XB[0:rows(full), full, :]).then_inc(out_written, 16)
                    writes += 1
            sp.wait_ge(out_written, 16 * writes)

        @block.gpsimd
        def _(pool):
            nc.gpsimd.memset(ident[:, :], 0.0).then_inc(id_zero, 1)
            pool.wait_ge(id_zero, 1)
            nc.gpsimd.affine_select(out=ident[:, :], in_=ident[:, :], compare_op=ALU.not_equal, fill=1.0,
                                    base=0, pattern=[[-1, P]], channel_multiplier=1).then_inc(id_ready, 1)
            def load_rows(c):
                pool.dma_start(A[0:rows(c), c, :], adj[c * P:c * P + rows(c), :]).then_inc(adj_in[c], 16)

            for c in range(4):
                load_rows(c)
            pool.wait_ge(x_peak, 4)
            nc.gpsimd.partition_all_reduce(peak_all[:, 4:5], peak[:, 4:5], P, bass.bass_isa.ReduceOp.max) \
                .then_inc(x_peak_all, 1)
            for c in range(4, NC):
                load_rows(c)

            pool.wait_ge(w_peak, 5)
            nc.gpsimd.partition_all_reduce(peak_all[:, 5:10], peak[:, 5:10], P, bass.bass_isa.ReduceOp.max) \
                .then_inc(w_peak_all, 1)

            def lowered(n, w, hi):
                pool.wait_ge(w_hi, n)
                nc.gpsimd.tensor_scalar(w, hi, 1.0 / LO, None, ALU.mult).then_inc(w_p, 1)

            lowered(1, Wp[:, 4, :], Wh[:, 4, :])
            lowered(2, Wp[:, 5, :], Wh[:, 5, :])

            for c in range(NC):
                r = rows(c)
                pool.wait_ge(relu_ready, c + 1)
                nc.gpsimd.tensor_tensor(X[0:r, c, :], X[0:r, c, :], relu[0:r, c, :], ALU.add) \
                    .then_inc(res_ready, 1)
            lowered(split_count(("outw", 0)), Op[:, :, :], Oh[:, :, :])
            for k in range(4):
                lowered(split_count(("fuse", k)), Wp[:, k, :], Wh[:, k, :])

            pool.wait_ge(job_ps, len(JOBS))
            pool.wait_ge(bias_in, 16 * 7)
            for c in range(NC):
                r = rows(c)
                pool.wait_ge(x1_ready, c + 1)
                nc.gpsimd.tensor_tensor(XB[0:r, c, :], X[0:r, c, :], b_o2[0:r, :], ALU.add) \
                  .then_inc(xb_ready, 1)

        @block.tensor
        def _(pe):
            mm = nc.tensor.matmul

            def adj_transposes(j):
                rj = rows(j)
                pe.wait_ge(adj_in[j], 16)
                if j >= 1:
                    pe.wait_ge(at_sbA, j)
                    if 0 <= j - 3 < 4:
                        pe.wait_ge(gate_T, j - 2)
                    elif 4 <= j - 3 < KC:
                        pe.wait_ge(w_lo, j - 6)
                for i in range(6):
                    ins = nc.tensor.transpose(ps16(6)[:, i * P:i * P + rj], A[0:rj, j, i * P:(i + 1) * P],
                                              ident16[0:rj, 0:rj])
                ins.then_inc(at_psA, 1)
                if j >= 1:
                    pe.wait_ge(at_sbB, 2 * j)
                for i in range(6, NC):
                    ri = rows(i)
                    ins = nc.tensor.transpose(ps16(7)[0:ri, (i - 6) * P:(i - 6) * P + rj],
                                              A[0:rj, j, i * P:i * P + ri], ident16[0:rj, 0:rj])
                ins.then_inc(at_psB, 1)

            def row_products(j, pairs):
                rj = rows(j)
                for part in range(2):
                    for h, t in pairs:
                        a, n = TILES[t]
                        ins = mm(ps[:, 2 * t + h, 0:n], XHL[0:rj, part, j, h * P:(h + 1) * P], A[0:rj, j, a:a + n],
                                 start=(j == 0 and part == 0), stop=(j == NC - 1 and part == 1),
                                 skip_group_check=True)
                return ins

            def column_sums(j):
                rj = rows(j)
                for i in range(NC):
                    ri = rows(i)
                    mm(ps[0:ri, CDEG_BANK, CDEG_AT + i:CDEG_AT + i + 1], A[0:rj, j, i * P:i * P + ri],
                       ones16[0:rj, :], start=False, stop=(j == NC - 1), skip_group_check=True)

            def gate_transposes(kc):
                if kc == 0:
                    pe.wait_ge(gates_in, 16 * 3)
                pe.wait_ge(at_sbA, kc + 3)
                pe.wait_ge(at_sbB, 2 * (kc + 3))
                for m in range(M6):
                    ins = nc.tensor.transpose(ps[:, 6 + m // 3, (m % 3) * P:(m % 3 + 1) * P],
                                              gates_raw[:, m, kc * P:(kc + 1) * P], ident[:, :])
                ins.then_inc(gate_ps, 1)

            pe.wait_ge(id_ready, 1)
            pe.wait_ge(id16_ready, 1)
            pe.wait_ge(ones_ready, 1)
            adj_transposes(0)
            for j in range(NC - 1):
                pe.wait_ge(x_hi, x_parts(j))
                pe.wait_ge(x_lo, x_parts(j))
                row_products(j, [(0, 0), (0, 1), (0, 2)])
                if 2 <= j < 2 + KC:
                    gate_transposes(j - 2)
                row_products(j, [(1, 0), (1, 1), (1, 2)])
                column_sums(j)
                adj_transposes(j + 1)
            column_sums(NC - 1)
            for t in range(NT):
                row_products(NC - 1, [(0, t), (1, t)]).then_inc(sum_done, 1)

            pe.wait_ge(w0_in, 16)
            pe.wait_ge(at_sbA, NC)
            pe.wait_ge(at_sbB, 2 * NC)
            for c in range(NC):
                r = rows(c)
                if c == 0:
                    pe.wait_ge(sum_act, 1)
                elif c == CPT:
                    pe.wait_ge(sum_dve, 1)
                elif c == 6:
                    pe.wait_ge(sum_act, 2)
                    pe.wait_ge(cdeg_ready, 2)
                elif c >= 8:
                    pe.wait_ge(relu_ready, c - 7)
                for k in range(H):
                    ins = mm(ps[0:r, L0_BANK[c], 0:D], Sm[:, k, c * P:c * P + r], w0_sb[:, k, :],
                             start=(k == 0), stop=(k == H - 1))
                ins.then_inc(l0_done, 1)

            pe.wait_ge(io_in, 16 * 4)
            pe.wait_ge(gate_T, 4)
            for j, (kind, k) in enumerate(JOBS):
                b = PAIRS[j % 4]
                if j < 4:
                    pe.wait_ge(relu_ready, L0_READ[j])
                elif JOBS[j - 4][0] != "state":
                    pe.wait_ge(w_lo, split_count(JOBS[j - 4]))
                else:
                    pe.wait_ge(sm_ready, JOBS[j - 4][1] + 1)
                if kind == "fuse":
                    w, kh = divmod(k, H)
                    for hf in range(2):
                        for m in range(H):
                            ins = mm(ps[:, b + hf, 0:G // 2], io_W[:, w, m, kh * P:(kh + 1) * P],
                                     gT[:, w * H + m, hf * G // 2:(hf + 1) * G // 2],
                                     start=(m == 0), stop=(m == H - 1))
                elif kind == "outw":
                    for w in range(2):
                        for kk in range(H):
                            for m in range(H):
                                ins = nc.tensor.transpose(
                                    ps[:, b + w, kk * D + m * P:kk * D + (m + 1) * P],
                                    o_W[:, w, m, kk * P:(kk + 1) * P], ident[:, :])
                else:
                    for c in chunks(k):
                        r = rows(c)
                        pe.wait_ge(x1_ready, c + 1)
                        for hf in range(H):
                            ins = nc.tensor.transpose(ps[:, b + hf, (c % CPT) * P:(c % CPT) * P + r],
                                                      X[0:r, c, hf * P:(hf + 1) * P], ident[0:r, 0:r])
                ins.then_inc(job_ps, 1)
            pe.wait_ge(w_lo, split_count(JOBS[-1]))
            pe.wait_ge(sm_ready, NT)

            def neighbours(t, ks, first, last, drained=None):
                a, n = TILES[t]
                for g in range(2 * H):
                    adjacency = AT if g < H else A
                    f = (g % H) * P
                    if drained is not None and g % H == 0:
                        pe.wait_ge(uv_hi, drained + g // H)
                        pe.wait_ge(uv_lo, drained + g // H)
                    for k in ks:
                        r = rows(k)
                        for part in (SnH, SnL):
                            ins = mm(ps[:, AGG + g, 0:n], part[0:r, k, f:f + P], adjacency[0:r, k, a:a + n],
                                     start=(first and k == ks[0] and part is SnH),
                                     stop=(last and k == ks[-1] and part is SnL))
                    if last and g % H == H - 1:
                        ins.then_inc(agg_done, 1)

            def gate_products(t, q, m, kcs, first, last):
                a, n = TILES[t]
                col = (q * H + m) * P
                for kc in kcs:
                    if kc < 2 * H:
                        hi, lo = UVH[:, kc, a:a + n], UVL[:, kc, a:a + n]
                    elif q < 2:
                        hi, lo = SfH[:, kc - 2 * H, a:a + n], SfL[:, kc - 2 * H, a:a + n]
                    else:
                        hi, lo = rsH[:, kc - 2 * H, 0:n], rsL[:, kc - 2 * H, 0:n]
                    for w, v in ((Wh, hi), (Wl, hi), (Wp, lo)):
                        ins = mm(ps[:, BANK[t][q] + m, 0:n], w[:, kc, col:col + P], v,
                                 start=(first and kc == kcs[0] and w is Wh),
                                 stop=(last and kc == kcs[-1] and w is Wp))
                return ins

            def state_transposes(t, hi_ready, lo_ready):
                for i, (part, ready) in enumerate(((SfH, hi_ready), (SfL, lo_ready))):
                    pe.wait_ge(*ready)
                    for c in chunks(t):
                        r = rows(c)
                        for hf in range(H):
                            at = (c % CPT) * D + hf * P
                            ins = nc.tensor.transpose(ps16(TBANK[t] + i)[0:r, at:at + P],
                                                      part[:, hf, c * P:c * P + r], ident16[:, :])
                    ins.then_inc(tn_ps, 1)

            def gates(t, st, between=None):
                for q in range(2):
                    for m in range(H):
                        ins = gate_products(t, q, m, range(KC), True, True)
                    ins.then_inc(gate_done[q], 1)
                if between:
                    between()
                if t < 2:
                    pe.wait_ge(gate_pre[0], 2 * NT * st + 2 * t + 2)
                else:
                    pe.wait_ge(gate_pre[1], 2 * NT * st + 2 * t)
                for m in range(H):
                    gate_products(t, 2, m, range(2 * H), True, False)
                pe.wait_ge(rs_hi, NT * st + t + 1)
                pe.wait_ge(rs_lo, NT * st + t + 1)
                for m in range(H):
                    ins = gate_products(t, 2, m, range(2 * H, KC), False, True)
                ins.then_inc(gate_done[2], 1)

            with pe.Fori(0, STEPS) as st:
                pe.wait_ge(tn_hi, 4 * st + 2)
                pe.wait_ge(tn_lo, 4 * st + 2)
                neighbours(0, range(0, 2 * CPT - 2), True, False)
                state_transposes(2, (s_hi, NT * st + 3), (s_lo, NT * st + 3))
                neighbours(0, range(2 * CPT - 2, 2 * CPT), False, False)
                pe.wait_ge(tn_hi, 4 * st + 4)
                pe.wait_ge(tn_lo, 4 * st + 4)
                neighbours(0, range(2 * CPT, NC), False, True)
                neighbours(1, range(NC), True, True, 6 * st + 1)
                pe.wait_ge(w_p, split_count(JOBS[-1]))
                pe.wait_ge(w_lo, split_count(JOBS[-1]))
                pe.wait_ge(uv_hi, 6 * st + 2)
                pe.wait_ge(uv_lo, 6 * st + 2)
                gates(0, st)
                neighbours(2, range(NC), True, True, 6 * st + 3)
                pe.wait_ge(uv_hi, 6 * st + 5)
                pe.wait_ge(uv_lo, 6 * st + 5)
                state_transposes(0, (s_hi, NT * st + 4), (s_lo, NT * st + 4))
                gates(1, st)
                pe.wait_ge(tn_hi, 4 * st + 5)
                pe.wait_ge(tn_lo, 4 * st + 5)
                pe.wait_ge(uv_hi, 6 * st + 6)
                pe.wait_ge(uv_lo, 6 * st + 6)
                gates(2, st, lambda: state_transposes(1, (s_hi, NT * st + 5), (s_lo, NT * st + 5)))

            O1_BANK = (0, 4, 6)
            O2_BANK = (2, 0, 4)

            def out1(t):
                a, n = TILES[t]
                for m in range(H):
                    for kk in range(H):
                        for w, v in ((Oh, SfH), (Ol, SfH), (Op, SfL)):
                            ins = mm(ps[:, O1_BANK[t] + m, 0:n], w[:, kk, m * P:(m + 1) * P],
                                     v[:, kk, a:a + n], start=(kk == 0 and w is Oh),
                                     stop=(kk == H - 1 and w is Op))
                ins.then_inc(o1_done, 1)

            def out2(t):
                pe.wait_ge(t_hi, t + 1)
                pe.wait_ge(t_lo, t + 1)
                for c in chunks(t):
                    r = rows(c)
                    bank, at = O2_BANK[t] + (c % CPT) // 2, (c % 2) * D
                    for kk in range(H):
                        for v, w in ((TH, Oh), (TH, Ol), (TL, Op)):
                            ins = mm(ps[0:r, bank, at:at + D], v[:, kk, c * P:c * P + r], w[:, H + kk, :],
                                     start=(kk == 0 and w is Oh), stop=(kk == H - 1 and w is Op))
                    ins.then_inc(o2_done, 1)

            pe.wait_ge(tn_hi, 4 * STEPS + 2)
            pe.wait_ge(tn_lo, 4 * STEPS + 2)
            out1(0)
            out1(1)
            pe.wait_ge(s_hi, NT * STEPS + 3)
            pe.wait_ge(s_lo, NT * STEPS + 3)
            out1(2)
            out2(0)
            pe.wait_ge(tanh_ready, 4)
            out2(1)
            out2(2)

        @block.scalar
        def _(act):
            def copy(o, i, scale=1.0):
                return nc.scalar.activation(o, i, ACT.Copy, scale=scale)

            with nc.allow_non_contiguous_dma(reason="biases become columns, once"):
                for q, b in enumerate((r_b, z_b, h_b)):
                    act.dma_start(b_gate[:, q * H:(q + 1) * H], b.rearrange("(k p) -> p k", p=P)) \
                       .then_inc(bias_in, 16)
                act.dma_start(b_o1[:, :], o1_b.rearrange("(k p) -> p k", p=P)).then_inc(bias_in, 16)
            for i, b in enumerate((in_b, out_b)):
                act.dma_start(b_in[:, i, :], b.rearrange("(a d) -> a d", a=1).to_broadcast([P, D])) \
                   .then_inc(bias_in, 16)
            act.dma_start(b_o2[:, :], o2_b.rearrange("(a d) -> a d", a=1).to_broadcast([P, D])).then_inc(bias_in, 16)

            act.wait_ge(x_scale, 4)
            for g, (c0, c1) in enumerate(XG):
                runs = [(P, c0, min(c1, NF))] + ([(rows(NF), NF, c1)] if c1 > NF else [])
                for r, a, b in runs:
                    copy(XHL[0:r, 0, a:b, :], X[0:r, a:b, :], xscale[0:r, 0:1]).then_inc(x_hi, 1)

            def gate_sixth(kc):
                act.wait_ge(gate_ps, kc + 1)
                both = ps[:, 6:8, 0:G // 2]
                if kc < 4:
                    copy(gT[:, kc, :].rearrange("p (a g) -> p a g", a=2), both).then_inc(gate_T, 1)
                else:
                    if kc == 4:
                        act.wait_ge(w_scale, 4)
                    copy(Wh[:, kc, :].rearrange("p (a g) -> p a g", a=2), both, wscale[:, 0:1]).then_inc(w_hi, 1)

            for j in range(NC):
                rj = rows(j)
                act.wait_ge(at_psA, j + 1)
                copy(AT[:, 0:6, j * P:j * P + rj],
                     ps16(6)[:, 0:6 * P].rearrange("p (i n) -> p i n", i=6)[:, :, 0:rj]).then_inc(at_sbA, 1)
                if 2 <= j < 2 + KC:
                    gate_sixth(j - 2)

            for t in (0, 2):
                a, n = TILES[t]
                act.wait_ge(sum_done, t + 1)
                copy(Sm[:, :, a:a + n], ps[:, 2 * t:2 * t + 2, 0:n]).then_inc(sum_act, 1)

            def roots(t, mv_done, done):
                for r, c0, c1 in column_runs(t):
                    act.wait_ge(mv_done, t + 1 + (c1 > NF))
                    nc.scalar.activation(rstd[0:r, c0:c1], newton[0:r, 0, c0:c1], ACT.Sqrt).then_inc(done, 1)

            act.wait_ge(clip_ready, 2)
            for r, c0, c1 in ((P, 0, NF), (rows(NF), NF, NC)):
                nc.scalar.activation(norm[0:r, c0:c1], newton[0:r, 0, c0:c1], ACT.Sqrt).then_inc(norm_root, 1)
            act.wait_ge(norm_ready, 1)
            for c in range(NC):
                r = rows(c)
                act.wait_ge(l0_done, c + 1)
                nc.scalar.activation(relu[0:r, c, :], ps[0:r, L0_BANK[c], 0:D],
                                     ACT.Relu, scale=norm[0:r, c:c + 1]).then_inc(relu_ready, 1)
                if c == 2 * CPT - 1:
                    roots(0, mv_ready, std_ready)

            for j, (kind, k) in enumerate(JOBS):
                b = PAIRS[j % 4]
                if kind == "state":
                    a, n = TILES[k]
                    if k < 2:
                        roots(k + 1, mv_ready, std_ready)
                        cs = chunks(k)
                        act.wait_ge(x1_ready, cs[-1] + 1)
                        copy(SnH[:, cs[0]:cs[-1] + 1, :], X[:, cs[0]:cs[-1] + 1, :], LO).then_inc(tn_hi, 1)
                    act.wait_ge(job_ps, j + 1)
                    copy(SfH[:, :, a:a + n], ps[:, b:b + 2, 0:n]).then_inc(s_hi, 1)
                    copy(Sm[:, :, a:a + n], ps[:, b:b + 2, 0:n], LO).then_inc(sm_ready, 1)
                elif kind == "fuse":
                    act.wait_ge(job_ps, j + 1)
                    copy(Wh[:, k, :].rearrange("p (a g) -> p a g", a=2), ps[:, b:b + 2, 0:G // 2],
                         wscale[:, 0:1]).then_inc(w_hi, 1)
                else:
                    act.wait_ge(job_ps, j + 1)
                    copy(Oh[:, :, :].rearrange("p a d -> p (a d)"),
                         ps[:, b:b + 2, :].rearrange("p a n -> p (a n)"), wscale[:, 0:1]).then_inc(w_hi, 1)

            def neighbours_hi(t, st):
                a, n = TILES[t]
                for s in range(2):
                    act.wait_ge(agg_done, 6 * st + 2 * t + s + 1)
                    copy(UVH[:, s * H:(s + 1) * H, a:a + n], ps[:, AGG + s * H:AGG + (s + 1) * H, 0:n], 1 / LO) \
                        .then_inc(uv_hi, 1)

            def gate(t, st, q, buf, func):
                a, n = TILES[t]
                for m in range(H):
                    act.wait_ge(gate_pre[q], 2 * NT * st + 2 * t + m + 1)
                    nc.scalar.activation(buf[:, m, 0:n], buf[:, m, 0:n], func, scale=wscale[:, 1:2],
                                         bias=b_gate[:, q * H + m:q * H + m + 1]).then_inc(gate_act[q], 1)

            def gates(t, st, before_h=None):
                a, n = TILES[t]
                gate(t, st, 0, gR, ACT.Sigmoid)
                act.wait_ge(rs_m, NT * st + t + 1)
                copy(rsH[:, :, 0:n], gR[:, :, 0:n], 1 / LO).then_inc(rs_hi, 1)
                gate(t, st, 1, gZ, ACT.Sigmoid)
                if before_h:
                    before_h()
                gate(t, st, 2, gH, ACT.Tanh)
                act.wait_ge(upd, 3 * NT * st + 3 * t + 3)
                copy(SfH[:, :, a:a + n], Sm[:, :, a:a + n], 1 / LO).then_inc(s_hi, 1)

            def state_nodes(t, count):
                act.wait_ge(tn_ps, count)
                c0, full = chunks(t)[0], min(chunks(t)[-1] + 1, NF)
                nf = full - c0
                copy(SnH[:, c0:full, :], ps16(TBANK[t])[:, 0:nf * D].rearrange("p (c d) -> p c d", c=nf), LO) \
                    .then_inc(tn_hi, 1)
                if full <= chunks(t)[-1]:
                    r = rows(full)
                    copy(SnH[0:r, full, :], ps16(TBANK[t])[0:r, nf * D:(nf + 1) * D], LO).then_inc(tn_hi, 1)

            with act.Fori(0, STEPS) as st:
                state_nodes(2, 6 * st + 1)
                neighbours_hi(0, st)
                neighbours_hi(1, st)
                gates(0, st)
                neighbours_hi(2, st)
                state_nodes(0, 6 * st + 3)
                gates(1, st)
                gates(2, st, lambda: state_nodes(1, 6 * st + 5))

            for t in range(NT):
                a, n = TILES[t]
                act.wait_ge(o1_done, t + 1)
                for m in range(H):
                    nc.scalar.activation(Tm[:, m, a:a + n], ps[:, (0, 4, 6)[t] + m, 0:n], ACT.Tanh,
                                         scale=wscale[:, 1:2], bias=b_o1[:, m:m + 1]).then_inc(tanh_ready, 1)
                act.wait_ge(tm_ready, t + 1)
                copy(TH[:, :, a:a + n], Tm[:, :, a:a + n], 1 / LO).then_inc(t_hi, 1)
            for t in range(NT):
                roots(t, mv2_ready, std2_ready)

        @block.vector
        def _(dve):
            nc.vector.memset(ones16[:, :], 1.0).then_inc(ones_ready, 1)

            def low(o, hi, full):
                return nc.vector.scalar_tensor_tensor(out=o, in0=hi, scalar=-LO, in1=full,
                                                      op0=ALU.mult, op1=ALU.add)

            dve.wait_ge(id_ready, 1)
            nc.vector.tensor_copy(ident16[:, :], ident[:, :]).then_inc(id16_ready, 1)

            def scales(out2, src, done):
                tmp = out2[:, 1:2]
                nc.vector.tensor_scalar(tmp.bitcast(I32), src.bitcast(I32), EXPONENT, None, ALU.bitwise_and) \
                    .then_inc(done, 1)
                dve.wait_ge(done, 1)
                nc.vector.tensor_scalar(tmp, tmp, LEAST, 1 / TOP, ALU.max, ALU.mult).then_inc(done, 1)
                dve.wait_ge(done, 2)
                nc.vector.reciprocal(out2[:, 0:1], tmp).then_inc(done, 2)

            nc.vector.memset(peak[:, :], 0.0).then_inc(x_peak, 1)
            dve.wait_ge(x_peak, 1)
            for g, (c0, c1) in enumerate(XG):
                dve.wait_ge(x_in[g], 16 * (1 + (c1 > NF)))
                full = min(c1, NF)
                nc.vector.tensor_reduce(peak[:, g:g + 1], X[:, c0:full, :], AX_XY, ALU.max,
                                        apply_absolute_value=True).then_inc(x_peak_part, 1)
            nc.vector.tensor_reduce(peak[0:rows(NF), 3:4], X[0:rows(NF), NF, :], AX_X, ALU.max,
                                    apply_absolute_value=True).then_inc(x_peak_part, 1)
            dve.wait_ge(x_peak_part, 4)
            nc.vector.tensor_reduce(peak[:, 4:5], peak[:, 0:4], AX_X, ALU.max).then_inc(x_peak, 3)
            dve.wait_ge(x_peak_all, 1)
            scales(xscale, peak_all[:, 4:5], x_scale)

            dve.wait_ge(x_scale, 4)
            for g, (c0, c1) in enumerate(XG):
                dve.wait_ge(x_hi, x_parts(c0))
                runs = [(P, c0, min(c1, NF))] + ([(rows(NF), NF, c1)] if c1 > NF else [])
                for r, a, b in runs:
                    nc.vector.scalar_tensor_tensor(out=XHL[0:r, 1, a:b, :], in0=X[0:r, a:b, :],
                                                   scalar=xscale[0:r, 0:1], in1=XHL[0:r, 0, a:b, :],
                                                   op0=ALU.mult, op1=ALU.subtract).then_inc(x_lo, 1)

            def gate_peak(q):
                if q == 0:
                    dve.wait_ge(gates_in, 16 * 3)
                nc.vector.tensor_reduce(peak[:, 5 + q:6 + q], gates_raw[:, q * H:(q + 1) * H, :], AX_XY, ALU.max,
                                        apply_absolute_value=True).then_inc(w_peak, 1)

            def other_peaks():
                dve.wait_ge(io_in, 16 * 4)
                for i, pair in enumerate((io_W, o_W)):
                    nc.vector.tensor_reduce(peak[:, 8 + i:9 + i], pair.rearrange("p w k m -> p (w k m)"), AX_X,
                                            ALU.max, apply_absolute_value=True).then_inc(w_peak, 1)

            def weight_scale():
                dve.wait_ge(w_peak_all, 1)
                nc.vector.tensor_reduce(peak_all[:, 5:6], peak_all[:, 5:8], AX_X, ALU.max).then_inc(w_max, 1)
                dve.wait_ge(w_max, 1)
                nc.vector.scalar_tensor_tensor(out=peak_all[:, 8:9], in0=peak_all[:, 8:9], scalar=float(D),
                                               in1=peak_all[:, 5:6], op0=ALU.mult, op1=ALU.mult).then_inc(w_max, 1)
                dve.wait_ge(w_max, 2)
                nc.vector.tensor_reduce(peak_all[:, 4:5], peak_all[:, 5:10], AX_X, ALU.max).then_inc(w_max, 1)
                dve.wait_ge(w_max, 3)
                scales(wscale, peak_all[:, 4:5], w_scale)

            def vectors(i):
                if i == 0:
                    dve.wait_ge(bias_in, 16 * 7)
                    dve.wait_ge(w_scale, 4)
                for n in range(i * 4, i * 4 + 4):
                    w, m = divmod(n, M6)
                    if n:
                        dve.wait_ge(v_ready, n)
                    nc.vector.tensor_tensor_reduce(junk[:, :], gates_raw[:, m, w * D:(w + 1) * D], b_in[:, w, :],
                                                   wscale[:, 0:1], 0.0, ALU.mult, ALU.add, v_gate[:, w, m:m + 1]) \
                        .then_inc(v_ready, 1)

            EXTRA = {1: lambda: gate_peak(0), 2: lambda: gate_peak(1), 3: lambda: gate_peak(2), 4: other_peaks,
                     5: weight_scale, 8: lambda: vectors(0), 9: lambda: vectors(1), 10: lambda: vectors(2)}
            for j in range(NC):
                rj = rows(j)
                dve.wait_ge(at_psB, j + 1)
                four = ps16(7)[:, 0:(NF - 6) * P].rearrange("p (i n) -> p i n", i=NF - 6)
                nc.vector.tensor_copy(AT[:, 6:NF, j * P:j * P + rj], four[:, :, 0:rj]).then_inc(at_sbB, 1)
                rl = rows(NF)
                nc.vector.tensor_copy(AT[0:rl, NF, j * P:j * P + rj],
                                      ps16(7)[0:rl, (NF - 6) * P:(NF - 6) * P + rj]).then_inc(at_sbB, 1)
                if j in (6, 7):
                    kc = j - 2
                    dve.wait_ge(w_hi, kc - 3)
                    nc.vector.scalar_tensor_tensor(
                        out=Wl[:, kc, :].rearrange("p (a g) -> p a g", a=2), in0=ps[:, 6:8, 0:G // 2],
                        scalar=wscale[:, 0:1], in1=Wh[:, kc, :].rearrange("p (a g) -> p a g", a=2),
                        op0=ALU.mult, op1=ALU.subtract).then_inc(w_lo, 1)
                nc.vector.tensor_reduce(rdeg[0:rj, j:j + 1], A[0:rj, j, :], AX_X, ALU.add).then_inc(rdeg_ready, 1)
                if j in EXTRA:
                    EXTRA[j]()

            dve.wait_ge(sum_done, 2)
            a, n = TILES[1]
            nc.vector.tensor_copy(Sm[:, :, a:a + n], ps[:, 2:4, 0:n]).then_inc(sum_dve, 1)
            dve.wait_ge(sum_done, 3)
            dve.wait_ge(sum_act, 2)
            rl = rows(NF)
            for r, a, b in ((P, 0, NF), (rl, NF, NC)):
                nc.vector.tensor_copy(cdeg[0:r, a:b], ps[0:r, CDEG_BANK, CDEG_AT + a:CDEG_AT + b]) \
                    .then_inc(cdeg_ready, 1)
            dve.wait_ge(cdeg_ready, 2)

            steps = [0]

            def exact_roots(y, v, r, c0, c1):
                y, v, w = y[0:r, c0:c1], v[0:r, 0, c0:c1], v[0:r, 1, c0:c1]

                def link(ins):
                    steps[0] += 1
                    ins.then_inc(nw_step, 1)
                    dve.wait_ge(nw_step, steps[0])

                link(nc.vector.reciprocal(y, y))
                link(nc.vector.tensor_tensor(w, y, y, ALU.mult))
                link(nc.vector.scalar_tensor_tensor(out=w, in0=w, scalar=-0.5, in1=v, op0=ALU.mult, op1=ALU.mult))
                return nc.vector.scalar_tensor_tensor(out=y, in0=w, scalar=1.5, in1=y, op0=ALU.add, op1=ALU.mult)

            for r, a, b in ((P, 0, NF), (rl, NF, NC)):
                nc.vector.tensor_scalar(newton[0:r, 0, a:b], cdeg[0:r, a:b], 1.0, None, ALU.max) \
                    .then_inc(clip_ready, 1)
            dve.wait_ge(norm_root, 2)
            for i, (r, a, b) in enumerate(((P, 0, NF), (rl, NF, NC))):
                exact_roots(norm, newton, r, a, b).then_inc(norm_exact, 1)
            dve.wait_ge(norm_exact, 2)
            nc.vector.tensor_scalar(norm[:, 0:NF], norm[:, 0:NF], xscale[:, 1:2], None, ALU.mult).then_inc(norm_exact, 1)
            dve.wait_ge(norm_exact, 3)
            nc.vector.tensor_scalar(norm[0:rl, NF:NC], norm[0:rl, NF:NC], xscale[0:rl, 1:2], None, ALU.mult) \
                .then_inc(norm_ready, 1)

            def layer_norm(t, src, dst, sems):
                s_stat, s_mv, s_var, s_std, s_rstd, s_out = sems
                cs = chunks(t)
                for c in cs:
                    nc.vector.bn_stats(stats[0:rows(c), c, :], src[0:rows(c), c, :]).then_inc(s_stat, 1)
                for c in cs:
                    dve.wait_ge(s_stat, c + 1)
                    nc.vector.bn_aggr(mv[0:rows(c), c, :], stats[0:rows(c), c, :]).then_inc(s_mv, 1)
                for r, c0, c1 in column_runs(t):
                    dve.wait_ge(s_mv, c1)
                    nc.vector.tensor_scalar(newton[0:r, 0, c0:c1], mv[0:r, c0:c1, 1], EPS, None, ALU.add) \
                        .then_inc(s_var, 1)
                for r, c0, c1 in column_runs(t):
                    dve.wait_ge(s_std, t + 1 + (c1 > NF))
                    exact_roots(rstd, newton, r, c0, c1).then_inc(s_rstd, 1)
                for c in cs:
                    r = rows(c)
                    dve.wait_ge(s_rstd, t + 1 + (c >= NF))
                    nc.vector.tensor_scalar(dst[0:r, c, :], src[0:r, c, :], mv[0:r, c, 0:1], rstd[0:r, c:c + 1],
                                            ALU.subtract, ALU.mult).then_inc(s_out, 1)

            def first_norm(t):
                dve.wait_ge(res_ready, chunks(t)[-1] + 1)
                layer_norm(t, X, X, (stat_ready, agg_ready, mv_ready, std_ready, rstd_ready, x1_ready))

            def fused_low(j, k):
                b = PAIRS[j % 4]
                dve.wait_ge(w_hi, split_count(JOBS[j]))
                if JOBS[j][0] == "fuse":
                    o, hi, full = (Wl[:, k, :].rearrange("p (a g) -> p a g", a=2),
                                   Wh[:, k, :].rearrange("p (a g) -> p a g", a=2), ps[:, b:b + 2, 0:G // 2])
                else:
                    o, hi, full = (Ol[:, :, :].rearrange("p a d -> p (a d)"), Oh[:, :, :].rearrange("p a d -> p (a d)"),
                                   ps[:, b:b + 2, :].rearrange("p a n -> p (a n)"))
                nc.vector.scalar_tensor_tensor(out=o, in0=full, scalar=wscale[:, 0:1], in1=hi,
                                               op0=ALU.mult, op1=ALU.subtract).then_inc(w_lo, 1)

            def first_state(t):
                a, n = TILES[t]
                if t < 2:
                    dve.wait_ge(tn_hi, t + 1)
                    c0, c1 = chunks(t)[0], chunks(t)[-1] + 1
                    nc.vector.scalar_tensor_tensor(
                        out=SnL[:, c0:c1, :], in0=X[:, c0:c1, :], scalar=LO, in1=SnH[:, c0:c1, :],
                        op0=ALU.mult, op1=ALU.subtract).then_inc(tn_lo, 1)
                dve.wait_ge(sm_ready, t + 1)
                dve.wait_ge(s_hi, t + 1)
                low(SfL[:, :, a:a + n], SfH[:, :, a:a + n], Sm[:, :, a:a + n]).then_inc(s_lo, 1)

            first_norm(0)
            for j, (kind, k) in enumerate(JOBS):
                if kind == "state":
                    if k < 2:
                        first_norm(k + 1)
                    first_state(k)
                else:
                    fused_low(j, k)

            def neighbours_lo(t, st):
                a, n = TILES[t]
                for s in range(2):
                    dve.wait_ge(uv_hi, 6 * st + 2 * t + s + 1)
                    low(UVL[:, s * H:(s + 1) * H, a:a + n], UVH[:, s * H:(s + 1) * H, a:a + n],
                        ps[:, AGG + s * H:AGG + (s + 1) * H, 0:n]).then_inc(uv_lo, 1)

            def gate(t, st, q, buf):
                a, n = TILES[t]
                dve.wait_ge(gate_done[q], NT * st + t + 1)
                for m in range(H):
                    nc.vector.scalar_tensor_tensor(
                        out=buf[:, m, 0:n], in0=Dr[:, a:a + n], scalar=v_gate[:, 0, q * H + m:q * H + m + 1],
                        in1=ps[:, BANK[t][q] + m, 0:n], op0=ALU.mult, op1=ALU.add).then_inc(gate_sum, 1)
                for m in range(H):
                    dve.wait_ge(gate_sum, 6 * NT * st + 6 * t + 2 * q + m + 1)
                    nc.vector.scalar_tensor_tensor(
                        out=buf[:, m, 0:n], in0=Dc[:, a:a + n], scalar=v_gate[:, 1, q * H + m:q * H + m + 1],
                        in1=buf[:, m, 0:n], op0=ALU.mult, op1=ALU.add).then_inc(gate_pre[q], 1)

            def gates(t, st, before_h=None):
                a, n = TILES[t]
                gate(t, st, 0, gR)
                dve.wait_ge(gate_act[0], 2 * NT * st + 2 * t + 2)
                nc.vector.tensor_tensor(gR[:, :, 0:n], gR[:, :, 0:n], Sm[:, :, a:a + n], ALU.mult) \
                    .then_inc(rs_m, 1)
                dve.wait_ge(rs_hi, NT * st + t + 1)
                low(rsL[:, :, 0:n], rsH[:, :, 0:n], gR[:, :, 0:n]).then_inc(rs_lo, 1)
                gate(t, st, 1, gZ)
                if before_h:
                    before_h()
                gate(t, st, 2, gH)
                dve.wait_ge(gate_act[2], 2 * NT * st + 2 * t + 2)
                nc.vector.scalar_tensor_tensor(out=gH[:, :, 0:n], in0=gH[:, :, 0:n], scalar=LO,
                                               in1=Sm[:, :, a:a + n], op0=ALU.mult,
                                               op1=ALU.subtract).then_inc(upd, 1)
                dve.wait_ge(gate_act[1], 2 * NT * st + 2 * t + 2)
                dve.wait_ge(upd, 3 * NT * st + 3 * t + 1)
                nc.vector.tensor_tensor(gH[:, :, 0:n], gH[:, :, 0:n], gZ[:, :, 0:n], ALU.mult).then_inc(upd, 1)
                dve.wait_ge(upd, 3 * NT * st + 3 * t + 2)
                nc.vector.tensor_tensor(Sm[:, :, a:a + n], Sm[:, :, a:a + n], gH[:, :, 0:n], ALU.add) \
                    .then_inc(upd, 1)
                dve.wait_ge(s_hi, NT * st + 3 + t + 1)
                low(SfL[:, :, a:a + n], SfH[:, :, a:a + n], Sm[:, :, a:a + n]).then_inc(s_lo, 1)

            def state_nodes(t, count):
                dve.wait_ge(tn_ps, count)
                c0, full = chunks(t)[0], min(chunks(t)[-1] + 1, NF)
                nf = full - c0
                b = ps16(TBANK[t] + 1)
                nc.vector.tensor_copy(SnL[:, c0:full, :], b[:, 0:nf * D].rearrange("p (c d) -> p c d", c=nf)) \
                    .then_inc(tn_lo, 1)
                if full <= chunks(t)[-1]:
                    r = rows(full)
                    nc.vector.tensor_copy(SnL[0:r, full, :], b[0:r, nf * D:(nf + 1) * D]).then_inc(tn_lo, 1)

            dve.wait_ge(deg_in, 32)
            dve.wait_ge(v_ready, 2 * M6)
            with dve.Fori(0, STEPS) as st:
                state_nodes(2, 6 * st + 2)
                neighbours_lo(0, st)
                neighbours_lo(1, st)
                gates(0, st)
                neighbours_lo(2, st)
                state_nodes(0, 6 * st + 4)
                gates(1, st)
                gates(2, st, lambda: state_nodes(1, 6 * st + 6))

            def split_tanh(t):
                a, n = TILES[t]
                dve.wait_ge(tanh_ready, 2 * t + 2)
                nc.vector.tensor_scalar(Tm[:, :, a:a + n], Tm[:, :, a:a + n], LO, None, ALU.mult) \
                    .then_inc(tm_ready, 1)
                dve.wait_ge(t_hi, t + 1)
                low(TL[:, :, a:a + n], TH[:, :, a:a + n], Tm[:, :, a:a + n]).then_inc(t_lo, 1)

            def last_norm(t):
                for c in chunks(t):
                    r = rows(c)
                    bank, at = (2, 0, 4)[t] + (c % CPT) // 2, (c % 2) * D
                    dve.wait_ge(o2_done, min(c // 2 * 2 + 2, NC))
                    dve.wait_ge(xb_ready, c + 1)
                    nc.vector.scalar_tensor_tensor(out=XB[0:r, c, :], in0=ps[0:r, bank, at:at + D],
                                                   scalar=wscale[0:r, 1:2],
                                                   in1=XB[0:r, c, :], op0=ALU.mult, op1=ALU.add) \
                        .then_inc(y2_ready, 1)
                dve.wait_ge(y2_ready, chunks(t)[-1] + 1)
                layer_norm(t, XB, XB, (st2_ready, agg2_ready, mv2_ready, std2_ready, rstd2_ready, out_ready))

            for t in range(NT):
                split_tanh(t)
            for t in range(NT):
                last_norm(t)


_INS = ['x', 'adj', 'L0_gnn_weight', 'L1_gnn_in_W', 'L1_gnn_in_b', 'L1_gnn_out_W', 'L1_gnn_out_b',
        'L1_gnn_r_W', 'L1_gnn_r_b', 'L1_gnn_z_W', 'L1_gnn_z_b', 'L1_gnn_h_W', 'L1_gnn_h_b',
        'L1_gnn_o1_W', 'L1_gnn_o1_b', 'L1_gnn_o2_W', 'L1_gnn_o2_b']


def kernel(**inputs):
    import numpy as _np
    import concourse.bacc as _bacc
    from concourse import mybir as _mybir
    from concourse.bass_utils import run_bass_kernel_spmd as _run

    nc = _bacc.Bacc("TRN2", target_bir_lowering=False, num_devices=1)
    arrays, args = {}, []
    for name in _INS:
        a = _np.ascontiguousarray(inputs[name])
        arrays[f"in_{name}_dram"] = a
        args.append(nc.dram_tensor(f"in_{name}_dram", a.shape, _mybir.dt.from_np(a.dtype),
                                   kind="ExternalInput").ap())
    shape = _np.asarray(inputs['x']).shape
    args.append(nc.dram_tensor("out_0_dram", shape, _mybir.dt.float32, kind="ExternalOutput").ap())
    gated_graph_net(nc, *args)
    r = _run(nc, [arrays], core_ids=[0])
    return r.results[0]["out_0_dram"]
```

```python
from contextlib import ExitStack

import concourse.bass as bass
from concourse import mybir

ALU = mybir.AluOpType
ACT = mybir.ActivationFunctionType
AX_X = mybir.AxisListType.X
AX_XY = mybir.AxisListType.XY
F32 = mybir.dt.float32
F16 = mybir.dt.float16
I32 = mybir.dt.int32

P = 128
STEPS = 5
EPS = 1e-5
LO = 2048.0
TOP = 2.0 ** 14
LEAST = 2.0 ** -60
EXPONENT = 0x7F800000


def gated_graph_net(nc: bass.Bass, x, adj, w0, in_W, in_b, out_W, out_b, r_W, r_b, z_W, z_b,
                    h_W, h_b, o1_W, o1_b, o2_W, o2_b, out):
    N, D = x.shape
    NC = -(-N // P)
    NF = N // P
    H = D // P
    TW = 512
    TILES = [(a, min(TW, N - a)) for a in range(0, N, TW)]
    NT = len(TILES)
    CPT = TW // P
    KC = 3 * H
    M6 = 3 * H
    G = M6 * P
    assert H == 2 and NT == 3 and NC == 11 and r_W.shape == (D, 3 * D)

    def rows(c):
        return min(P, N - c * P)

    def chunks(t):
        return range(t * CPT, min((t + 1) * CPT, NC))

    def column_runs(t):
        c0, c1 = chunks(t)[0], chunks(t)[-1] + 1
        return [(P, c0, min(c1, NF))] + ([(rows(NF), NF, c1)] if c1 > NF else [])

    with ExitStack() as ctx:
        def sb(name, shape, dt=F32):
            return ctx.enter_context(nc.sbuf_tensor(name, shape, dt))

        def sem(name):
            return ctx.enter_context(nc.semaphore(name))

        A = sb("A", [P, NC, N], F16)
        AT = sb("AT", [P, NC, N], F16)
        X = sb("X", [P, NC, D])
        SnH = sb("SnH", [P, NC, D], F16)
        SnL = sb("SnL", [P, NC, D], F16)
        Sm = sb("Sm", [P, H, N])
        Wh = sb("Wh", [P, KC, G], F16)
        Wl = sb("Wl", [P, KC, G], F16)
        Wp = sb("Wp", [P, KC, G], F16)
        Oh = sb("Oh", [P, 2 * H, D], F16)
        Ol = sb("Ol", [P, 2 * H, D], F16)
        Op = sb("Op", [P, H, D], F16)
        ident = sb("ident", [P, P])
        ident16 = sb("ident16", [P, P], F16)
        b_gate = sb("b_gate", [P, M6])
        b_o1 = sb("b_o1", [P, H])
        b_o2 = sb("b_o2", [P, D])
        v_gate = sb("v_gate", [P, 2, M6])
        rdeg = sb("rdeg", [P, NC])
        cdeg = sb("cdeg", [P, NC])
        cdeg_parts = sb("cdeg_parts", [P, NC, NC])
        norm = sb("norm", [P, NC])
        stats = sb("stats", [P, NC, 6])
        mv = sb("mv", [P, NC, 2])
        rstd = sb("rstd", [P, NC])
        shift = sb("shift", [P, 2 * CPT])
        newton = sb("newton", [P, 2, NC])
        peak = sb("peak", [P, 10])
        peak_all = sb("peak_all", [P, 10])
        junk = sb("junk", [P, D])
        xscale = sb("xscale", [P, 2])
        wscale = sb("wscale", [P, 3])

        uv = sb("uv", [P, 4 * N])
        UVH = uv[:, 0:2 * N].bitcast(F16).rearrange("p (k n) -> p k n", k=2 * H)
        UVL = uv[:, 2 * N:4 * N].bitcast(F16).rearrange("p (k n) -> p k n", k=2 * H)
        gates_raw = uv[:, 0:3 * H * 3 * D].rearrange("p (k m) -> p k m", k=3 * H)
        b_in = uv[:, 9 * H * D:9 * H * D + 2 * D].rearrange("p (w d) -> p w d", w=2)
        TH, TL = UVH[:, 0:H], UVL[:, 0:H]
        Tm = X[:, :, :].rearrange("p c d -> p (c d)")[:, 0:H * N].rearrange("p (k n) -> p k n", k=H)

        act_mem = sb("act_mem", [P, 4 * H * TW])
        gR, gZ, gH = (act_mem[:, q * H * TW:(q + 1) * H * TW].rearrange("p (k n) -> p k n", k=H)
                      for q in range(3))
        rs_mem = act_mem[:, 3 * H * TW:4 * H * TW].bitcast(F16).rearrange("p (s k n) -> p s k n", s=2, k=H)
        rsH, rsL = rs_mem[:, 0], rs_mem[:, 1]
        relu = act_mem[:, 0:NC * D].rearrange("p (c d) -> p c d", c=NC)
        XHL = act_mem[:, 0:NC * D].bitcast(F16).rearrange("p (s c d) -> p s c d", s=2, c=NC)

        gt_mem = sb("gt_mem", [P, 4 * G])
        gT = gt_mem[:, :].rearrange("p (k g) -> p k g", k=4)
        XB = gt_mem[:, 0:NC * D].rearrange("p (c d) -> p c d", c=NC)

        sf_mem = sb("sf_mem", [P, 2 * N])
        SfH = sf_mem[:, 0:N].bitcast(F16).rearrange("p (k n) -> p k n", k=H)
        SfL = sf_mem[:, N:2 * N].bitcast(F16).rearrange("p (k n) -> p k n", k=H)
        w0_sb = sf_mem[:, 0:2 * D].rearrange("p (k m) -> p k m", k=H)

        Dr = sb("Dr", [P, N])
        Dc = sb("Dc", [P, N])
        row_copy = Dr[:, 0:N // 2].bitcast(F16)
        io_W = act_mem[:, NC * D:NC * D + 4 * D].rearrange("p (w k m) -> p w k m", w=2, k=H)
        o_W = Dc[:, 0:4 * D].rearrange("p (w k m) -> p w k m", w=2, k=H)
        deg_rows = nc.dram_tensor("deg_rows", [2, N], F32).ap()

        ps = ctx.enter_context(nc.psum_tensor("ps", [P, 8, TW], F32))

        def ps16(b):
            return ps[:, b, :].bitcast(F16)

        XG = [(0, 4), (4, 8), (8, NC)]
        XS = [(0, 1), (1, 3), (3, 6), (6, NC)]

        x_in = [sem(f"x_in{i}") for i in range(3)]
        adj_in = [sem(f"adj_in{c}") for c in range(NC)]
        w0_in = sem("w0_in")
        gates_in = sem("gates_in")
        io_in = sem("io_in")
        bias_in = sem("bias_in")
        at_zero = sem("at_zero")
        mv_zero = sem("mv_zero")
        cdeg_part = sem("cdeg_part")
        id_zero = sem("id_zero")
        id_ready = sem("id_ready")
        id16_ready = sem("id16_ready")
        x_peak = sem("x_peak")
        x_peak_all = sem("x_peak_all")
        x_scale = sem("x_scale")
        w_peak = sem("w_peak")
        w_peak_all = sem("w_peak_all")
        w_scale = sem("w_scale")
        v_ready = sem("v_ready")
        x_hi = sem("x_hi")
        x_lo = sem("x_lo")
        at_psA = sem("at_psA")
        at_psB = sem("at_psB")
        at_sbA = sem("at_sbA")
        at_sbB = sem("at_sbB")
        gate_ps = sem("gate_ps")
        gate_T = sem("gate_T")
        sum_done = sem("sum_done")
        sum_read = sem("sum_read")
        l0_done = sem("l0_done")
        rdeg_ready = sem("rdeg_ready")
        cdeg_ready = sem("cdeg_ready")
        norm_ready = sem("norm_ready")
        relu_ready = sem("relu_ready")
        res_ready = sem("res_ready")
        stat_ready = sem("stat_ready")
        mv_part = sem("mv_part")
        mv2_part = sem("mv2_part")
        norm_exact = sem("norm_exact")
        x_peak_part = sem("x_peak_part")
        w_max = sem("w_max")
        mv_ready = sem("mv_ready")
        clip_ready = sem("clip_ready")
        norm_root = sem("norm_root")
        std_ready = sem("std_ready")
        rstd_ready = sem("rstd_ready")
        x1_ready = sem("x1_ready")
        job_ps = sem("job_ps")
        w_hi = sem("w_hi")
        w_lo = sem("w_lo")
        w_p = sem("w_p")
        sm_ready = sem("sm_ready")
        deg_out = sem("deg_out")
        deg_in = sem("deg_in")
        nw_step = sem("nw_step")
        xb_ready = sem("xb_ready")
        agg_done = sem("agg_done")
        uv_hi = sem("uv_hi")
        uv_lo = sem("uv_lo")
        gate_done = [sem(f"{g}_done") for g in "rzh"]
        gate_sum = sem("gate_sum")
        gate_pre = [sem(f"{g}_pre") for g in "rzh"]
        gate_act = [sem(f"{g}_act") for g in "rzh"]
        rs_m = sem("rs_m")
        rs_hi = sem("rs_hi")
        rs_lo = sem("rs_lo")
        upd = sem("upd")
        s_hi = sem("s_hi")
        s_lo = sem("s_lo")
        tn_ps = sem("tn_ps")
        tn_hi = sem("tn_hi")
        tn_lo = sem("tn_lo")
        o1_done = sem("o1_done")
        tanh_ready = sem("tanh_ready")
        shift_ready = sem("shift_ready")
        t_hi = sem("t_hi")
        t_lo = sem("t_lo")
        o2_done = sem("o2_done")
        y2_ready = sem("y2_ready")
        st2_ready = sem("st2_ready")
        mv2_ready = sem("mv2_ready")
        std2_ready = sem("std2_ready")
        rstd2_ready = sem("rstd2_ready")
        out_ready = sem("out_ready")
        last_ready = sem("last_ready")
        out_written = sem("out_written")

        AHEAD, GATES_FROM = 2, 5
        L0_BANK = [(6 + c) % 8 for c in range(NC)]
        JOBS = [("fuse", 0), ("fuse", 1), ("fuse", 2), ("state", 0), ("fuse", 3), ("state", 1),
                ("state", 2), ("outw", 0)]
        PAIRS = [2, 4, 6, 0, 2, 0, 2, 0]
        L0_READ = [6, 8, 10, NC]

        def x_parts(c):
            g = [i for i, (a, b) in enumerate(XS) if a <= c < b][0]
            return g + 1 + (XS[g][1] > NF)

        def x_runs(g):
            a, b = XS[g]
            return [(P, a, min(b, NF))] + ([(rows(NF), NF, b)] if b > NF else [])

        def split_count(job):
            return 4 + [j for j in JOBS if j[0] != "state"].index(job) + 1

        AGG = 4
        BANK = {0: (0, 2, 0), 1: (0, 2, 0), 2: (4, 6, 2)}
        TBANK = {0: 4, 1: 0, 2: 0}
        O1_BANK = (4, 0, 4)
        O2_BANK = (6, 0, 2)

        block = ctx.enter_context(nc.Block())

        @block.sync
        def _(sp):
            sp.dma_start(X[0:rows(NF), NF, :], x[NF * P:N, :]).then_inc(x_in[2], 16)
            for g, (a, b) in enumerate(XG):
                full = min(b, NF)
                sp.dma_start(X[:, a:full, :], x[a * P:full * P, :].rearrange("(c p) d -> p c d", p=P)) \
                  .then_inc(x_in[g], 16)
                if g == 2:
                    sp.dma_start(w0_sb[:, :, :], w0.rearrange("(k p) m -> p k m", p=P)).then_inc(w0_in, 16)
            sp.wait_ge(adj_in[2], 16)
            for q, w in enumerate((r_W, z_W, h_W)):
                sp.dma_start(gates_raw[:, q * H:(q + 1) * H, :], w.rearrange("(k p) m -> p k m", p=P)) \
                  .then_inc(gates_in, 16)
            for place, w in ((io_W[:, 0], in_W), (io_W[:, 1], out_W), (o_W[:, 0], o1_W), (o_W[:, 1], o2_W)):
                sp.dma_start(place, w.rearrange("(k p) m -> p k m", p=P)).then_inc(io_in, 16)

            sp.wait_ge(rdeg_ready, NC)
            sp.wait_ge(cdeg_ready, 1)
            with nc.allow_non_contiguous_dma(reason="columns become rows, once"):
                for i, d in enumerate((rdeg, cdeg)):
                    sp.dma_start(deg_rows[i, 0:NF * P].rearrange("(c p) -> p c", p=P), d[:, 0:NF]) \
                      .then_inc(deg_out, 16)
                    sp.dma_start(deg_rows[i, NF * P:N].rearrange("(c p) -> p c", c=1), d[0:rows(NF), NF:NC]) \
                      .then_inc(deg_out, 16)
            sp.wait_ge(deg_out, 64)
            sp.dma_start(Dr[:, :], deg_rows[0:1, :].to_broadcast([P, N])).then_inc(deg_in, 16)
            sp.wait_ge(job_ps, JOBS.index(("outw", 0)) + 1)
            sp.dma_start(Dc[:, :], deg_rows[1:2, :].to_broadcast([P, N])).then_inc(deg_in, 16)

            pieces = [(0, 2), (2, 4), (4, 6), (6, 8), (8, NC)]
            for a, b in pieces:
                full = min(b, NF)
                if b <= 2 * CPT:
                    sp.wait_ge(out_ready, b)
                else:
                    sp.wait_ge(last_ready, b - a)
                sp.dma_start(out[a * P:full * P, :].rearrange("(c p) d -> p c d", p=P), XB[:, a:full, :]) \
                  .then_inc(out_written, 16)
            sp.dma_start(out[NF * P:N, :], XB[0:rows(NF), NF, :]).then_inc(out_written, 16)
            writes = len(pieces) + 1
            sp.wait_ge(out_written, 16 * writes)

        @block.gpsimd
        def _(pool):
            nc.gpsimd.memset(ident[:, :], 0.0).then_inc(id_zero, 1)
            pool.wait_ge(id_zero, 1)
            nc.gpsimd.affine_select(out=ident[:, :], in_=ident[:, :], compare_op=ALU.not_equal, fill=1.0,
                                    base=0, pattern=[[-1, P]], channel_multiplier=1).then_inc(id_ready, 1)

            def load_rows(c):
                pool.dma_start(A[0:rows(c), c, :], adj[c * P:c * P + rows(c), :]).then_inc(adj_in[c], 16)

            load_rows(0)
            pool.wait_ge(x_in[1], 16)
            load_rows(1)
            load_rows(2)
            pool.wait_ge(x_peak, 4)
            nc.gpsimd.partition_all_reduce(peak_all[:, 4:5], peak[:, 4:5], P, bass.bass_isa.ReduceOp.max) \
                .then_inc(x_peak_all, 1)
            for c in range(3, NC):
                load_rows(c)

            pool.wait_ge(w_peak, 5)
            nc.gpsimd.partition_all_reduce(peak_all[:, 5:10], peak[:, 5:10], P, bass.bass_isa.ReduceOp.max) \
                .then_inc(w_peak_all, 1)

            def lowered(n, w, hi):
                pool.wait_ge(w_hi, n)
                nc.gpsimd.tensor_scalar(w, hi, 1.0 / LO, None, ALU.mult).then_inc(w_p, 1)

            lowered(2, Wp[:, 4, :], Wh[:, 4, :])
            lowered(4, Wp[:, 5, :], Wh[:, 5, :])

            for c in range(NC):
                r = rows(c)
                pool.wait_ge(relu_ready, c + 1)
                nc.gpsimd.tensor_tensor(X[0:r, c, :], X[0:r, c, :], relu[0:r, c, :], ALU.add) \
                    .then_inc(res_ready, 1)
            for k in range(4):
                lowered(split_count(("fuse", k)), Wp[:, k, :], Wh[:, k, :])
            lowered(split_count(("outw", 0)), Op[:, :H, :], Oh[:, :H, :])

            pool.wait_ge(job_ps, JOBS.index(("fuse", 3)) + 1)
            pool.wait_ge(bias_in, 16 * 7)
            for c in range(NC):
                r = rows(c)
                pool.wait_ge(x1_ready, c + 1)
                nc.gpsimd.tensor_tensor(XB[0:r, c, :], X[0:r, c, :], b_o2[0:r, :], ALU.add) \
                  .then_inc(xb_ready, 1)

        @block.tensor
        def _(pe):
            mm = nc.tensor.matmul

            def adj_transposes(j):
                rj = rows(j)
                pe.wait_ge(adj_in[j], 16)
                if j >= 1:
                    pe.wait_ge(at_sbA, j)
                    kc = j - 1 - GATES_FROM
                    if 0 <= kc < 4:
                        pe.wait_ge(gate_T, kc + 1)
                    elif 4 <= kc < KC:
                        pe.wait_ge(w_lo, 2 * kc - 7)
                for i in range(6):
                    ins = nc.tensor.transpose(ps16(6)[:, i * P:i * P + rj], A[0:rj, j, i * P:(i + 1) * P],
                                              ident16[0:rj, 0:rj])
                ins.then_inc(at_psA, 1)
                if j >= 1:
                    pe.wait_ge(at_sbB, 2 * j)
                    if 4 <= j - 1 - GATES_FROM < KC:
                        pe.wait_ge(w_lo, 2 * (j - 1 - GATES_FROM) - 6)
                for i in range(6, NC):
                    ri = rows(i)
                    ins = nc.tensor.transpose(ps16(7)[0:ri, (i - 6) * P:(i - 6) * P + rj],
                                              A[0:rj, j, i * P:i * P + ri], ident16[0:rj, 0:rj])
                ins.then_inc(at_psB, 1)

            def row_products(j, pairs):
                rj = rows(j)
                for part in range(2):
                    for h, t in pairs:
                        a, n = TILES[t]
                        ins = mm(ps[:, 2 * t + h, 0:n], XHL[0:rj, part, j, h * P:(h + 1) * P], A[0:rj, j, a:a + n],
                                 start=(j == 0 and part == 0), stop=(j == NC - 1 and part == 1),
                                 skip_group_check=True)
                return ins

            def gate_transposes(kc):
                if kc == 0:
                    pe.wait_ge(gates_in, 16 * 3)
                pe.wait_ge(at_sbA, GATES_FROM + kc + 1)
                pe.wait_ge(at_sbB, 2 * (GATES_FROM + kc + 1))
                for m in range(M6):
                    ins = nc.tensor.transpose(ps[:, 6 + m // 3, (m % 3) * P:(m % 3 + 1) * P],
                                              gates_raw[:, m, kc * P:(kc + 1) * P], ident[:, :])
                ins.then_inc(gate_ps, 1)

            pe.wait_ge(id_ready, 1)
            pe.wait_ge(id16_ready, 1)
            for j in range(AHEAD):
                adj_transposes(j)
            for j in range(NC - 1):
                pe.wait_ge(x_hi, x_parts(j))
                pe.wait_ge(x_lo, x_parts(j))
                row_products(j, [(0, 0), (0, 1), (0, 2)])
                if 0 <= j + AHEAD - 1 - GATES_FROM < KC:
                    gate_transposes(j + AHEAD - 1 - GATES_FROM)
                row_products(j, [(1, 0), (1, 1), (1, 2)])
                if j + AHEAD < NC:
                    adj_transposes(j + AHEAD)
            for t in range(NT):
                row_products(NC - 1, [(0, t), (1, t)]).then_inc(sum_done, 1)

            pe.wait_ge(w0_in, 16)
            pe.wait_ge(at_sbA, NC)
            pe.wait_ge(at_sbB, 2 * NC)
            pe.wait_ge(w_lo, 4)
            for c in range(NC):
                r = rows(c)
                if c % CPT == 0:
                    pe.wait_ge(sum_read, c // CPT + 1)
                if L0_BANK[c] == 4:
                    pe.wait_ge(sum_read, 3)
                if c >= 8:
                    pe.wait_ge(relu_ready, c - 7)
                for k in range(H):
                    ins = mm(ps[0:r, L0_BANK[c], 0:D], Sm[:, k, c * P:c * P + r], w0_sb[:, k, :],
                             start=(k == 0), stop=(k == H - 1))
                ins.then_inc(l0_done, 1)

            pe.wait_ge(io_in, 16 * 4)
            pe.wait_ge(gate_T, 4)

            def job(kind, k):
                j = JOBS.index((kind, k))
                b = PAIRS[j]
                if j < 4:
                    pe.wait_ge(relu_ready, L0_READ[j])
                else:
                    before = JOBS[max(i for i in range(j) if PAIRS[i] == b)]
                    if before[0] == "state":
                        pe.wait_ge(s_hi, before[1] + 1)
                    else:
                        pe.wait_ge(w_lo, split_count(before))
                if kind == "fuse":
                    w, kh = divmod(k, H)
                    for hf in range(2):
                        for m in range(H):
                            ins = mm(ps[:, b + hf, 0:G // 2], io_W[:, w, m, kh * P:(kh + 1) * P],
                                     gT[:, w * H + m, hf * G // 2:(hf + 1) * G // 2],
                                     start=(m == 0), stop=(m == H - 1))
                elif kind == "outw":
                    for w in range(2):
                        for kk in range(H):
                            for m in range(H):
                                ins = nc.tensor.transpose(
                                    ps[:, b + w, kk * D + m * P:kk * D + (m + 1) * P],
                                    o_W[:, w, m, kk * P:(kk + 1) * P], ident[:, :])
                else:
                    for c in chunks(k):
                        r = rows(c)
                        pe.wait_ge(x1_ready, c + 1)
                        for hf in range(H):
                            ins = nc.tensor.transpose(ps[:, b + hf, (c % CPT) * P:(c % CPT) * P + r],
                                                      X[0:r, c, hf * P:(hf + 1) * P], ident[0:r, 0:r])
                ins.then_inc(job_ps, 1)

            for j in JOBS[:5]:
                job(*j)

            def neighbours(t, ks, first, last, drained=None):
                a, n = TILES[t]
                for g in range(2 * H):
                    adjacency = AT if g < H else A
                    f = (g % H) * P
                    if drained is not None and g % H == 0:
                        pe.wait_ge(uv_hi, drained + g // H)
                        pe.wait_ge(uv_lo, drained + g // H)
                    for k in ks:
                        r = rows(k)
                        for part in (SnH, SnL):
                            ins = mm(ps[:, AGG + g, 0:n], part[0:r, k, f:f + P], adjacency[0:r, k, a:a + n],
                                     start=(first and k == ks[0] and part is SnH),
                                     stop=(last and k == ks[-1] and part is SnL))
                    if last and g % H == H - 1:
                        ins.then_inc(agg_done, 1)

            def gate_products(t, q, m, kcs, first, last):
                a, n = TILES[t]
                col = (q * H + m) * P
                for kc in kcs:
                    if kc < 2 * H:
                        hi, lo = UVH[:, kc, a:a + n], UVL[:, kc, a:a + n]
                    elif q < 2:
                        hi, lo = SfH[:, kc - 2 * H, a:a + n], SfL[:, kc - 2 * H, a:a + n]
                    else:
                        hi, lo = rsH[:, kc - 2 * H, 0:n], rsL[:, kc - 2 * H, 0:n]
                    for w, v in ((Wh, hi), (Wl, hi), (Wp, lo)):
                        ins = mm(ps[:, BANK[t][q] + m, 0:n], w[:, kc, col:col + P], v,
                                 start=(first and kc == kcs[0] and w is Wh),
                                 stop=(last and kc == kcs[-1] and w is Wp))
                return ins

            def state_transposes(t, hi_ready, lo_ready):
                for i, (part, ready) in enumerate(((SfH, hi_ready), (SfL, lo_ready))):
                    pe.wait_ge(*ready)
                    for c in chunks(t):
                        r = rows(c)
                        for hf in range(H):
                            at = (c % CPT) * D + hf * P
                            ins = nc.tensor.transpose(ps16(TBANK[t] + i)[0:r, at:at + P],
                                                      part[:, hf, c * P:c * P + r], ident16[:, :])
                    ins.then_inc(tn_ps, 1)

            def out1(t, st):
                pe.wait_ge(s_hi, NT * st + 4 + t)
                pe.wait_ge(s_lo, NT * st + 4 + t)
                a, n = TILES[t]
                for m in range(H):
                    for kk in range(H):
                        for w, v in ((Oh, SfH), (Ol, SfH), (Op, SfL)):
                            ins = mm(ps[:, O1_BANK[t] + m, 0:n], w[:, kk, m * P:(m + 1) * P],
                                     v[:, kk, a:a + n], start=(kk == 0 and w is Oh),
                                     stop=(kk == H - 1 and w is Op))
                ins.then_inc(o1_done, 1)

            def out2(t):
                pe.wait_ge(t_hi, t + 1)
                pe.wait_ge(t_lo, t + 1)
                for c in chunks(t):
                    r = rows(c)
                    bank, at = O2_BANK[t] + (c % CPT) // 2, (c % 2) * D
                    for kk in range(H):
                        for v, w in ((TH, Oh), (TH, Ol), (TL, Oh)):
                            ins = mm(ps[0:r, bank, at:at + D], v[:, kk, c * P:c * P + r], w[:, H + kk, :],
                                     start=(kk == 0 and w is Oh and v is TH), stop=(kk == H - 1 and v is TL))
                    ins.then_inc(o2_done, 1)

            def gates(t, st, last=False):
                for q in range(2):
                    for m in range(H):
                        ins = gate_products(t, q, m, range(KC), True, True)
                    ins.then_inc(gate_done[q], 1)
                if t < 2:
                    pe.wait_ge(gate_pre[0], 2 * NT * st + 2 * t + 2)
                else:
                    pe.wait_ge(gate_pre[1], 2 * NT * st + 2 * t)
                for m in range(H):
                    gate_products(t, 2, m, range(2 * H), True, False)
                if t == 2:
                    if last:
                        out1(1, st)
                    else:
                        state_transposes(1, (s_hi, NT * st + 5), (s_lo, NT * st + 5))
                    pe.wait_ge(gate_pre[1], 2 * NT * st + 2 * t + 2)
                pe.wait_ge(rs_hi, NT * st + t + 1)
                pe.wait_ge(rs_lo, NT * st + t + 1)
                for m in range(H):
                    ins = gate_products(t, 2, m, range(2 * H, KC), False, True)
                ins.then_inc(gate_done[2], 1)

            def step(st, first=False, last=False):
                if first:
                    pe.wait_ge(w_lo, split_count(("fuse", 2)))
                pe.wait_ge(tn_hi, 4 * st + 1)
                pe.wait_ge(tn_lo, 4 * st + 1)
                neighbours(0, range(0, CPT), True, False)
                if first:
                    job("state", 1)
                pe.wait_ge(tn_hi, 4 * st + 2)
                pe.wait_ge(tn_lo, 4 * st + 2)
                neighbours(0, range(CPT, 2 * CPT - 2), False, False)
                if not first:
                    state_transposes(2, (s_hi, NT * st + 3), (s_lo, NT * st + 3))
                neighbours(0, range(2 * CPT - 2, 2 * CPT), False, False)
                if first:
                    job("state", 2)
                    job("outw", 0)
                pe.wait_ge(tn_hi, 4 * st + 4)
                pe.wait_ge(tn_lo, 4 * st + 4)
                neighbours(0, range(2 * CPT, NC), False, True)
                neighbours(1, range(NC), True, True, 6 * st + 1)
                if first:
                    pe.wait_ge(s_hi, NT)
                    pe.wait_ge(s_lo, NT)
                    pe.wait_ge(w_p, KC + 1)
                    pe.wait_ge(w_lo, split_count(("outw", 0)))
                pe.wait_ge(uv_hi, 6 * st + 2)
                pe.wait_ge(uv_lo, 6 * st + 2)
                gates(0, st)
                neighbours(2, range(NC), True, True, 6 * st + 3)
                pe.wait_ge(uv_hi, 6 * st + 5)
                pe.wait_ge(uv_lo, 6 * st + 5)
                if last:
                    out1(0, st)
                else:
                    state_transposes(0, (s_hi, NT * st + 4), (s_lo, NT * st + 4))
                gates(1, st)
                if last:
                    pe.wait_ge(tanh_ready, 2)
                else:
                    pe.wait_ge(tn_hi, 4 * st + 5)
                    pe.wait_ge(tn_lo, 4 * st + 5)
                pe.wait_ge(uv_hi, 6 * st + 6)
                pe.wait_ge(uv_lo, 6 * st + 6)
                gates(2, st, last)

            step(0, first=True)
            with pe.Fori(1, STEPS - 1) as st:
                step(st)
            step(STEPS - 1, last=True)

            out2(0)
            out2(1)
            out1(2, STEPS - 1)
            out2(2)

        @block.scalar
        def _(act):
            def copy(o, i, scale=1.0):
                return nc.scalar.activation(o, i, ACT.Copy, scale=scale)

            def x_high(g):
                for r, a, b in x_runs(g):
                    copy(XHL[0:r, 0, a:b, :], X[0:r, a:b, :], xscale[0:r, 0:1]).then_inc(x_hi, 1)

            def half_transposed(j):
                rj = rows(j)
                act.wait_ge(at_psA, j + 1)
                copy(AT[:, 0:6, j * P:j * P + rj],
                     ps16(6)[:, 0:6 * P].rearrange("p (i n) -> p i n", i=6)[:, :, 0:rj]).then_inc(at_sbA, 1)

            def row_sums(j):
                rj = rows(j)
                if j:
                    act.wait_ge(rdeg_ready, j)
                act.wait_ge(adj_in[j], 16)
                nc.scalar.activation(row_copy[0:rj, :], A[0:rj, j, :], ACT.Copy,
                                     accum_out=rdeg[0:rj, j:j + 1]).then_inc(rdeg_ready, 1)

            def gate_sixth(kc):
                act.wait_ge(gate_ps, kc + 1)
                both = ps[:, 6:8, 0:G // 2]
                if kc < 4:
                    copy(gT[:, kc, :].rearrange("p (a g) -> p a g", a=2), both).then_inc(gate_T, 1)
                else:
                    if kc == 4:
                        act.wait_ge(w_scale, 5)
                    for a in range(2):
                        copy(Wh[:, kc, a * G // 2:(a + 1) * G // 2], ps[:, 6 + a, 0:G // 2], wscale[:, 0:1]) \
                            .then_inc(w_hi, 1)

            half_transposed(0)
            act.wait_ge(x_scale, 4)
            x_high(0)
            half_transposed(1)
            x_high(1)
            x_high(2)
            x_high(3)
            with nc.allow_non_contiguous_dma(reason="biases become columns, once"):
                for q, b in enumerate((r_b, z_b, h_b)):
                    act.dma_start(b_gate[:, q * H:(q + 1) * H], b.rearrange("(k p) -> p k", p=P)) \
                       .then_inc(bias_in, 16)
                act.dma_start(b_o1[:, :], o1_b.rearrange("(k p) -> p k", p=P)).then_inc(bias_in, 16)
            for i, b in enumerate((in_b, out_b)):
                act.dma_start(b_in[:, i, :], b.rearrange("(a d) -> a d", a=1).to_broadcast([P, D])) \
                   .then_inc(bias_in, 16)
            act.dma_start(b_o2[:, :], o2_b.rearrange("(a d) -> a d", a=1).to_broadcast([P, D])).then_inc(bias_in, 16)

            for j in range(AHEAD, NC):
                half_transposed(j)
                if 0 <= j - GATES_FROM < KC:
                    gate_sixth(j - GATES_FROM)
                row_sums(j - AHEAD)

            for t in range(NT):
                a, n = TILES[t]
                act.wait_ge(sum_done, t + 1)
                copy(Sm[:, :, a:a + n], ps[:, 2 * t:2 * t + 2, 0:n]).then_inc(sum_read, 1)

            row_sums(NC - 2)

            act.wait_ge(clip_ready, 1)
            nc.scalar.activation(norm[:, :], newton[:, 0, :], ACT.Sqrt).then_inc(norm_root, 1)
            row_sums(NC - 1)

            def roots(t, mv_done, done):
                c0, c1 = chunks(t)[0], chunks(t)[-1] + 1
                act.wait_ge(mv_done, t + 1)
                nc.scalar.activation(rstd[:, c0:c1], newton[:, 0, c0:c1], ACT.Sqrt).then_inc(done, 1)

            act.wait_ge(norm_ready, 1)
            for c in range(NC):
                r = rows(c)
                act.wait_ge(l0_done, c + 1)
                nc.scalar.activation(relu[0:r, c, :], ps[0:r, L0_BANK[c], 0:D],
                                     ACT.Relu, scale=norm[0:r, c:c + 1]).then_inc(relu_ready, 1)

            def weights_high(kind, k):
                j = JOBS.index((kind, k))
                b = PAIRS[j]
                act.wait_ge(job_ps, j + 1)
                if kind == "fuse":
                    o, full = Wh[:, k, :].rearrange("p (a g) -> p a g", a=2), ps[:, b:b + 2, 0:G // 2]
                else:
                    o, full = (Oh[:, :, :].rearrange("p a d -> p (a d)"),
                               ps[:, b:b + 2, :].rearrange("p a n -> p (a n)"))
                copy(o, full, wscale[:, 0:1]).then_inc(w_hi, 1)

            def first_nodes(t):
                act.wait_ge(x1_ready, chunks(t)[-1] + 1)
                for r, c0, c1 in column_runs(t):
                    copy(SnH[0:r, c0:c1, :], X[0:r, c0:c1, :], LO).then_inc(tn_hi, 1)

            def first_features(t):
                j = JOBS.index(("state", t))
                b = PAIRS[j]
                a, n = TILES[t]
                act.wait_ge(job_ps, j + 1)
                copy(Sm[:, :, a:a + n], ps[:, b:b + 2, 0:n], LO).then_inc(sm_ready, 1)
                copy(SfH[:, :, a:a + n], ps[:, b:b + 2, 0:n]).then_inc(s_hi, 1)

            roots(0, mv_ready, std_ready)
            weights_high("fuse", 0)
            first_nodes(0)
            weights_high("fuse", 1)
            weights_high("fuse", 2)
            first_features(0)
            roots(1, mv_ready, std_ready)
            weights_high("fuse", 3)
            first_nodes(1)
            roots(2, mv_ready, std_ready)
            first_nodes(2)
            first_features(1)
            first_features(2)
            weights_high("outw", 0)

            def neighbours_hi(t, st):
                a, n = TILES[t]
                for s in range(2):
                    act.wait_ge(agg_done, 6 * st + 2 * t + s + 1)
                    copy(UVH[:, s * H:(s + 1) * H, a:a + n], ps[:, AGG + s * H:AGG + (s + 1) * H, 0:n], 1 / LO) \
                        .then_inc(uv_hi, 1)

            def gate(t, st, q, buf, func):
                a, n = TILES[t]
                for m in range(H):
                    act.wait_ge(gate_pre[q], 2 * NT * st + 2 * t + m + 1)
                    nc.scalar.activation(buf[:, m, 0:n], buf[:, m, 0:n], func, scale=wscale[:, 1:2],
                                         bias=b_gate[:, q * H + m:q * H + m + 1]).then_inc(gate_act[q], 1)

            def split_rs(t, st):
                a, n = TILES[t]
                act.wait_ge(rs_m, NT * st + t + 1)
                copy(rsH[:, :, 0:n], gR[:, :, 0:n], 1 / LO).then_inc(rs_hi, 1)

            def split_state(t, st):
                a, n = TILES[t]
                act.wait_ge(upd, 3 * NT * st + 3 * t + 3)
                copy(SfH[:, :, a:a + n], Sm[:, :, a:a + n], 1 / LO).then_inc(s_hi, 1)

            def state_nodes(t, count):
                act.wait_ge(tn_ps, count)
                c0, full = chunks(t)[0], min(chunks(t)[-1] + 1, NF)
                nf = full - c0
                copy(SnH[:, c0:full, :], ps16(TBANK[t])[:, 0:nf * D].rearrange("p (c d) -> p c d", c=nf), LO) \
                    .then_inc(tn_hi, 1)
                if full <= chunks(t)[-1]:
                    r = rows(full)
                    copy(SnH[0:r, full, :], ps16(TBANK[t])[0:r, nf * D:(nf + 1) * D], LO).then_inc(tn_hi, 1)

            def tanh_out(t):
                a, n = TILES[t]
                act.wait_ge(o1_done, t + 1)
                for m in range(H):
                    nc.scalar.activation(Tm[:, m, a:a + n], ps[:, O1_BANK[t] + m, 0:n], ACT.Tanh,
                                         scale=wscale[:, 1:2], bias=b_o1[:, m:m + 1]).then_inc(tanh_ready, 1)
                act.wait_ge(tanh_ready, 2 * t + 2)
                copy(TH[:, :, a:a + n], Tm[:, :, a:a + n], LO).then_inc(t_hi, 1)

            def step(st, first=False, last=False):
                if first:
                    act.wait_ge(v_ready, 2 * M6)
                else:
                    state_nodes(2, 6 * st - 1)
                neighbours_hi(0, st)
                neighbours_hi(1, st)
                gate(0, st, 0, gR, ACT.Sigmoid)
                split_rs(0, st)
                gate(0, st, 1, gZ, ACT.Sigmoid)
                gate(0, st, 2, gH, ACT.Tanh)
                split_state(0, st)
                neighbours_hi(2, st)
                if last:
                    act.wait_ge(xb_ready, NC)
                    tanh_out(0)
                else:
                    state_nodes(0, 6 * st + 1)
                gate(1, st, 0, gR, ACT.Sigmoid)
                split_rs(1, st)
                gate(1, st, 1, gZ, ACT.Sigmoid)
                gate(1, st, 2, gH, ACT.Tanh)
                gate(2, st, 0, gR, ACT.Sigmoid)
                split_state(1, st)
                split_rs(2, st)
                gate(2, st, 1, gZ, ACT.Sigmoid)
                if last:
                    tanh_out(1)
                else:
                    state_nodes(1, 6 * st + 3)
                gate(2, st, 2, gH, ACT.Tanh)
                split_state(2, st)

            step(0, first=True)
            with act.Fori(1, STEPS - 1) as st:
                step(st)
            step(STEPS - 1, last=True)
            tanh_out(2)

            def normalised(cs):
                for c in cs:
                    act.wait_ge(shift_ready, 1)
                    nc.scalar.activation(XB[:, c, :], XB[:, c, :], ACT.Identity, scale=rstd[:, c:c + 1],
                                         bias=shift[:, c:c + 1]).then_inc(out_ready, 1)

            roots(0, mv2_ready, std2_ready)
            roots(1, mv2_ready, std2_ready)
            normalised(range(0, CPT + 2))
            roots(2, mv2_ready, std2_ready)
            normalised(range(CPT + 2, 2 * CPT))

        @block.vector
        def _(dve):
            def low(o, hi, full):
                return nc.vector.scalar_tensor_tensor(out=o, in0=hi, scalar=-LO, in1=full,
                                                      op0=ALU.mult, op1=ALU.add)

            dve.wait_ge(id_ready, 1)
            nc.vector.tensor_copy(ident16[:, :], ident[:, :]).then_inc(id16_ready, 1)

            def scales(out2, src, done):
                tmp = out2[:, 1:2]
                nc.vector.tensor_scalar(tmp.bitcast(I32), src.bitcast(I32), EXPONENT, None, ALU.bitwise_and) \
                    .then_inc(done, 1)
                dve.wait_ge(done, 1)
                nc.vector.tensor_scalar(tmp, tmp, LEAST, 1 / TOP, ALU.max, ALU.mult).then_inc(done, 1)
                dve.wait_ge(done, 2)
                nc.vector.reciprocal(out2[:, 0:1], tmp).then_inc(done, 2)

            nc.vector.memset(AT[:, NF, :], 0.0).then_inc(at_zero, 1)
            nc.vector.memset(mv[:, :, :], 0.0).then_inc(mv_zero, 1)
            nc.vector.memset(peak[:, :], 0.0).then_inc(x_peak, 1)
            dve.wait_ge(x_peak, 1)
            for g, (c0, c1) in enumerate(XG):
                dve.wait_ge(x_in[g], 16 * (1 + (c1 > NF)))
                full = min(c1, NF)
                nc.vector.tensor_reduce(peak[:, g:g + 1], X[:, c0:full, :], AX_XY, ALU.max,
                                        apply_absolute_value=True).then_inc(x_peak_part, 1)
            nc.vector.tensor_reduce(peak[0:rows(NF), 3:4], X[0:rows(NF), NF, :], AX_X, ALU.max,
                                    apply_absolute_value=True).then_inc(x_peak_part, 1)
            dve.wait_ge(x_peak_part, 4)
            nc.vector.tensor_reduce(peak[:, 4:5], peak[:, 0:4], AX_X, ALU.max).then_inc(x_peak, 3)

            def half_transposed(j):
                rj, rl = rows(j), rows(NF)
                dve.wait_ge(at_psB, j + 1)
                four = ps16(7)[:, 0:(NF - 6) * P].rearrange("p (i n) -> p i n", i=NF - 6)
                nc.vector.tensor_copy(AT[:, 6:NF, j * P:j * P + rj], four[:, :, 0:rj]).then_inc(at_sbB, 1)
                if j == 0:
                    dve.wait_ge(at_zero, 1)
                nc.vector.tensor_copy(AT[0:rl, NF, j * P:j * P + rj],
                                      ps16(7)[0:rl, (NF - 6) * P:(NF - 6) * P + rj]).then_inc(at_sbB, 1)

            def column_sums(j):
                dve.wait_ge(at_sbA, j + 1)
                dve.wait_ge(at_sbB, 2 * j + 2)
                nc.vector.tensor_reduce(cdeg_parts[:, :, j], AT[:, :, j * P:j * P + rows(j)], AX_X, ALU.add) \
                    .then_inc(cdeg_part, 1)

            def x_low(g):
                dve.wait_ge(x_hi, x_parts(XS[g][0]))
                for r, a, b in x_runs(g):
                    nc.vector.scalar_tensor_tensor(out=XHL[0:r, 1, a:b, :], in0=X[0:r, a:b, :],
                                                   scalar=xscale[0:r, 0:1], in1=XHL[0:r, 0, a:b, :],
                                                   op0=ALU.mult, op1=ALU.subtract).then_inc(x_lo, 1)

            half_transposed(0)
            dve.wait_ge(x_peak_all, 1)
            scales(xscale, peak_all[:, 4:5], x_scale)
            dve.wait_ge(x_scale, 4)
            x_low(0)
            half_transposed(1)
            x_low(1)
            x_low(2)
            x_low(3)

            def gate_peak(q):
                if q == 0:
                    dve.wait_ge(gates_in, 16 * 3)
                nc.vector.tensor_reduce(peak[:, 5 + q:6 + q], gates_raw[:, q * H:(q + 1) * H, :], AX_XY, ALU.max,
                                        apply_absolute_value=True).then_inc(w_peak, 1)

            def other_peaks():
                dve.wait_ge(io_in, 16 * 4)
                for i, pair in enumerate((io_W, o_W)):
                    nc.vector.tensor_reduce(peak[:, 8 + i:9 + i], pair.rearrange("p w k m -> p (w k m)"), AX_X,
                                            ALU.max, apply_absolute_value=True).then_inc(w_peak, 1)

            def weight_scale():
                dve.wait_ge(w_peak_all, 1)
                nc.vector.tensor_reduce(peak_all[:, 5:6], peak_all[:, 5:8], AX_X, ALU.max).then_inc(w_max, 1)
                dve.wait_ge(w_max, 1)
                nc.vector.scalar_tensor_tensor(out=peak_all[:, 8:9], in0=peak_all[:, 8:9], scalar=float(D),
                                               in1=peak_all[:, 5:6], op0=ALU.mult, op1=ALU.mult).then_inc(w_max, 1)
                dve.wait_ge(w_max, 2)
                nc.vector.tensor_reduce(peak_all[:, 4:5], peak_all[:, 5:10], AX_X, ALU.max).then_inc(w_max, 1)
                dve.wait_ge(w_max, 3)
                scales(wscale, peak_all[:, 4:5], w_scale)
                nc.vector.tensor_scalar(wscale[:, 2:3], wscale[:, 1:2], 1.0 / LO, None, ALU.mult).then_inc(w_scale, 1)

            def bias_vectors(first, end):
                for n in range(first, end):
                    w, m = divmod(n, M6)
                    if n:
                        dve.wait_ge(v_ready, n)
                    nc.vector.tensor_tensor_reduce(junk[:, :], gates_raw[:, m, w * D:(w + 1) * D], b_in[:, w, :],
                                                   wscale[:, 0:1], 0.0, ALU.mult, ALU.add, v_gate[:, w, m:m + 1]) \
                        .then_inc(v_ready, 1)

            SPARE = [lambda: column_sums(0), lambda: column_sums(1), lambda: gate_peak(0), lambda: gate_peak(1),
                     lambda: gate_peak(2), other_peaks, lambda: (weight_scale(), column_sums(2))]
            for j in range(AHEAD, NC):
                half_transposed(j)
                if j - GATES_FROM < 4:
                    SPARE[j - AHEAD]()
                else:
                    kc = j - GATES_FROM
                    column_sums(2 * kc - 5)
                    for a in range(2):
                        dve.wait_ge(w_hi, 2 * kc - 7 + a)
                        nc.vector.scalar_tensor_tensor(
                            out=Wl[:, kc, a * G // 2:(a + 1) * G // 2], in0=ps[:, 6 + a, 0:G // 2],
                            scalar=wscale[:, 0:1], in1=Wh[:, kc, a * G // 2:(a + 1) * G // 2],
                            op0=ALU.mult, op1=ALU.subtract).then_inc(w_lo, 1)
                    column_sums(2 * kc - 4)
            for j in range(7, NC):
                column_sums(j)

            links = [0]

            def exact_roots(y, v, c0, c1):
                y, v, w = y[:, c0:c1], v[:, 0, c0:c1], v[:, 1, c0:c1]

                def link(ins):
                    links[0] += 1
                    ins.then_inc(nw_step, 1)
                    dve.wait_ge(nw_step, links[0])

                link(nc.vector.reciprocal(y, y))
                link(nc.vector.tensor_tensor(w, y, y, ALU.mult))
                link(nc.vector.scalar_tensor_tensor(out=w, in0=w, scalar=-0.5, in1=v, op0=ALU.mult, op1=ALU.mult))
                return nc.vector.scalar_tensor_tensor(out=y, in0=w, scalar=1.5, in1=y, op0=ALU.add, op1=ALU.mult)

            dve.wait_ge(cdeg_part, NC)
            nc.vector.tensor_reduce(cdeg[:, :], cdeg_parts[:, :, :], AX_X, ALU.add).then_inc(cdeg_ready, 1)
            dve.wait_ge(cdeg_ready, 1)
            nc.vector.tensor_scalar(newton[:, 0, :], cdeg[:, :], 1.0, None, ALU.max).then_inc(clip_ready, 1)
            dve.wait_ge(norm_root, 1)
            exact_roots(norm, newton, 0, NC).then_inc(norm_exact, 1)
            dve.wait_ge(norm_exact, 1)
            nc.vector.tensor_scalar(norm[:, :], norm[:, :], xscale[:, 1:2], None, ALU.mult).then_inc(norm_ready, 1)

            def moments(t, src, s_stat, s_part, s_mv):
                cs = chunks(t)
                for c in cs:
                    nc.vector.bn_stats(stats[0:rows(c), c, :], src[0:rows(c), c, :]).then_inc(s_stat, 1)
                for c in cs:
                    dve.wait_ge(s_stat, c + 1)
                    nc.vector.bn_aggr(mv[0:rows(c), c, :], stats[0:rows(c), c, :]).then_inc(s_part, 1)
                dve.wait_ge(s_part, cs[-1] + 1)
                nc.vector.tensor_scalar(newton[:, 0, cs[0]:cs[-1] + 1], mv[:, cs[0]:cs[-1] + 1, 1], EPS, None,
                                        ALU.add).then_inc(s_mv, 1)

            def first_norm(t):
                dve.wait_ge(res_ready, chunks(t)[-1] + 1)
                moments(t, X, stat_ready, mv_part, mv_ready)
                dve.wait_ge(std_ready, t + 1)
                exact_roots(rstd, newton, chunks(t)[0], chunks(t)[-1] + 1).then_inc(rstd_ready, 1)
                for c in chunks(t):
                    r = rows(c)
                    dve.wait_ge(rstd_ready, t + 1)
                    nc.vector.tensor_scalar(X[0:r, c, :], X[0:r, c, :], mv[0:r, c, 0:1], rstd[0:r, c:c + 1],
                                            ALU.subtract, ALU.mult).then_inc(x1_ready, 1)

            def weights_low(kind, k):
                b = PAIRS[JOBS.index((kind, k))]
                dve.wait_ge(w_hi, split_count((kind, k)))
                if kind == "fuse":
                    o, hi, full = (Wl[:, k, :].rearrange("p (a g) -> p a g", a=2),
                                   Wh[:, k, :].rearrange("p (a g) -> p a g", a=2), ps[:, b:b + 2, 0:G // 2])
                else:
                    o, hi, full = (Ol[:, :, :].rearrange("p a d -> p (a d)"), Oh[:, :, :].rearrange("p a d -> p (a d)"),
                                   ps[:, b:b + 2, :].rearrange("p a n -> p (a n)"))
                nc.vector.scalar_tensor_tensor(out=o, in0=full, scalar=wscale[:, 0:1], in1=hi,
                                               op0=ALU.mult, op1=ALU.subtract).then_inc(w_lo, 1)

            def first_nodes(t):
                for r, c0, c1 in column_runs(t):
                    dve.wait_ge(tn_hi, t + 1 + (c1 > NF))
                    nc.vector.scalar_tensor_tensor(
                        out=SnL[0:r, c0:c1, :], in0=X[0:r, c0:c1, :], scalar=LO, in1=SnH[0:r, c0:c1, :],
                        op0=ALU.mult, op1=ALU.subtract).then_inc(tn_lo, 1)

            def first_features(t):
                a, n = TILES[t]
                dve.wait_ge(s_hi, t + 1)
                low(SfL[:, :, a:a + n], SfH[:, :, a:a + n], Sm[:, :, a:a + n]).then_inc(s_lo, 1)

            dve.wait_ge(bias_in, 16 * 7)
            dve.wait_ge(w_scale, 5)
            dve.wait_ge(mv_zero, 1)
            bias_vectors(0, 6)
            first_norm(0)
            weights_low("fuse", 0)
            first_nodes(0)
            weights_low("fuse", 1)
            bias_vectors(6, 9)
            weights_low("fuse", 2)
            first_norm(1)
            bias_vectors(9, 2 * M6)
            first_nodes(1)
            weights_low("fuse", 3)
            first_norm(2)
            first_nodes(2)
            first_features(0)
            first_features(1)
            first_features(2)
            weights_low("outw", 0)

            def neighbours_lo(t, st):
                a, n = TILES[t]
                for s in range(2):
                    dve.wait_ge(uv_hi, 6 * st + 2 * t + s + 1)
                    low(UVL[:, s * H:(s + 1) * H, a:a + n], UVH[:, s * H:(s + 1) * H, a:a + n],
                        ps[:, AGG + s * H:AGG + (s + 1) * H, 0:n]).then_inc(uv_lo, 1)

            def gate(t, st, q, buf):
                a, n = TILES[t]
                dve.wait_ge(gate_done[q], NT * st + t + 1)
                for m in range(H):
                    nc.vector.scalar_tensor_tensor(
                        out=buf[:, m, 0:n], in0=Dr[:, a:a + n], scalar=v_gate[:, 0, q * H + m:q * H + m + 1],
                        in1=ps[:, BANK[t][q] + m, 0:n], op0=ALU.mult, op1=ALU.add).then_inc(gate_sum, 1)
                for m in range(H):
                    dve.wait_ge(gate_sum, 6 * NT * st + 6 * t + 2 * q + m + 1)
                    nc.vector.scalar_tensor_tensor(
                        out=buf[:, m, 0:n], in0=Dc[:, a:a + n], scalar=v_gate[:, 1, q * H + m:q * H + m + 1],
                        in1=buf[:, m, 0:n], op0=ALU.mult, op1=ALU.add).then_inc(gate_pre[q], 1)

            def reset_product(t, st):
                a, n = TILES[t]
                dve.wait_ge(gate_act[0], 2 * NT * st + 2 * t + 2)
                nc.vector.tensor_tensor(gR[:, :, 0:n], gR[:, :, 0:n], Sm[:, :, a:a + n], ALU.mult) \
                    .then_inc(rs_m, 1)

            def split_rs(t, st):
                a, n = TILES[t]
                dve.wait_ge(rs_hi, NT * st + t + 1)
                low(rsL[:, :, 0:n], rsH[:, :, 0:n], gR[:, :, 0:n]).then_inc(rs_lo, 1)

            def difference(t, st):
                a, n = TILES[t]
                dve.wait_ge(gate_act[2], 2 * NT * st + 2 * t + 2)
                nc.vector.scalar_tensor_tensor(out=gH[:, :, 0:n], in0=gH[:, :, 0:n], scalar=LO,
                                               in1=Sm[:, :, a:a + n], op0=ALU.mult,
                                               op1=ALU.subtract).then_inc(upd, 1)

            def update(t, st):
                a, n = TILES[t]
                dve.wait_ge(gate_act[1], 2 * NT * st + 2 * t + 2)
                dve.wait_ge(upd, 3 * NT * st + 3 * t + 1)
                nc.vector.tensor_tensor(gH[:, :, 0:n], gH[:, :, 0:n], gZ[:, :, 0:n], ALU.mult).then_inc(upd, 1)
                dve.wait_ge(upd, 3 * NT * st + 3 * t + 2)
                nc.vector.tensor_tensor(Sm[:, :, a:a + n], Sm[:, :, a:a + n], gH[:, :, 0:n], ALU.add) \
                    .then_inc(upd, 1)

            def split_state(t, st):
                a, n = TILES[t]
                dve.wait_ge(s_hi, NT * st + 3 + t + 1)
                low(SfL[:, :, a:a + n], SfH[:, :, a:a + n], Sm[:, :, a:a + n]).then_inc(s_lo, 1)

            def state_nodes(t, count):
                dve.wait_ge(tn_ps, count)
                c0, full = chunks(t)[0], min(chunks(t)[-1] + 1, NF)
                nf = full - c0
                b = ps16(TBANK[t] + 1)
                nc.vector.tensor_copy(SnL[:, c0:full, :], b[:, 0:nf * D].rearrange("p (c d) -> p c d", c=nf)) \
                    .then_inc(tn_lo, 1)
                if full <= chunks(t)[-1]:
                    r = rows(full)
                    nc.vector.tensor_copy(SnL[0:r, full, :], b[0:r, nf * D:(nf + 1) * D]).then_inc(tn_lo, 1)

            def split_tanh(t):
                a, n = TILES[t]
                dve.wait_ge(t_hi, t + 1)
                nc.vector.scalar_tensor_tensor(out=TL[:, :, a:a + n], in0=Tm[:, :, a:a + n], scalar=LO,
                                               in1=TH[:, :, a:a + n], op0=ALU.mult, op1=ALU.subtract) \
                    .then_inc(t_lo, 1)

            def second_sum(*pairs):
                for i in pairs:
                    c0, c1 = 2 * i, min(2 * i + 2, NC)
                    r, t = rows(c1 - 1), c0 // CPT
                    bank = O2_BANK[t] + (c0 % CPT) // 2
                    dve.wait_ge(o2_done, c1)
                    dve.wait_ge(xb_ready, c1)
                    nc.vector.scalar_tensor_tensor(
                        out=XB[0:r, c0:c1, :], scalar=wscale[0:r, 2:3], in1=XB[0:r, c0:c1, :],
                        in0=ps[0:r, bank, 0:(c1 - c0) * D].rearrange("p (c d) -> p c d", c=c1 - c0),
                        op0=ALU.mult, op1=ALU.add).then_inc(y2_ready, 1)

            def step(st, first=False, last=False):
                if not first:
                    state_nodes(2, 6 * st)
                neighbours_lo(0, st)
                neighbours_lo(1, st)
                if first:
                    dve.wait_ge(deg_in, 32)
                    dve.wait_ge(v_ready, 2 * M6)
                gate(0, st, 0, gR)
                reset_product(0, st)
                split_rs(0, st)
                gate(0, st, 1, gZ)
                gate(0, st, 2, gH)
                difference(0, st)
                update(0, st)
                split_state(0, st)
                neighbours_lo(2, st)
                if last:
                    split_tanh(0)
                else:
                    state_nodes(0, 6 * st + 2)
                gate(1, st, 0, gR)
                reset_product(1, st)
                split_rs(1, st)
                gate(1, st, 1, gZ)
                gate(1, st, 2, gH)
                difference(1, st)
                gate(2, st, 0, gR)
                update(1, st)
                reset_product(2, st)
                split_rs(2, st)
                split_state(1, st)
                gate(2, st, 1, gZ)
                if not last:
                    state_nodes(1, 6 * st + 4)
                gate(2, st, 2, gH)
                if last:
                    split_tanh(1)
                difference(2, st)
                update(2, st)
                if last:
                    second_sum(0)
                split_state(2, st)

            step(0, first=True)
            with dve.Fori(1, STEPS - 1) as st:
                step(st)
            step(STEPS - 1, last=True)

            def second_moments(t):
                dve.wait_ge(y2_ready, 2 * t + 2)
                moments(t, XB, st2_ready, mv2_part, mv2_ready)

            second_sum(1)
            second_moments(0)
            second_sum(2, 3)
            split_tanh(2)
            second_moments(1)
            two = 2 * CPT
            dve.wait_ge(std2_ready, 2)
            exact_roots(rstd, newton, 0, two).then_inc(rstd2_ready, 1)
            dve.wait_ge(rstd2_ready, 1)
            nc.vector.scalar_tensor_tensor(out=shift[:, :], in0=mv[:, 0:two, 0], scalar=-1.0,
                                           in1=rstd[:, 0:two], op0=ALU.mult, op1=ALU.mult).then_inc(shift_ready, 1)
            second_sum(4, 5)
            second_moments(2)
            dve.wait_ge(std2_ready, NT)
            exact_roots(rstd, newton, two, NC).then_inc(rstd2_ready, 1)
            dve.wait_ge(rstd2_ready, 2)
            for c in chunks(2):
                r = rows(c)
                nc.vector.tensor_scalar(XB[0:r, c, :], XB[0:r, c, :], mv[0:r, c, 0:1], rstd[0:r, c:c + 1],
                                        ALU.subtract, ALU.mult).then_inc(last_ready, 1)


_INS = ['x', 'adj', 'L0_gnn_weight', 'L1_gnn_in_W', 'L1_gnn_in_b', 'L1_gnn_out_W', 'L1_gnn_out_b',
        'L1_gnn_r_W', 'L1_gnn_r_b', 'L1_gnn_z_W', 'L1_gnn_z_b', 'L1_gnn_h_W', 'L1_gnn_h_b',
        'L1_gnn_o1_W', 'L1_gnn_o1_b', 'L1_gnn_o2_W', 'L1_gnn_o2_b']


def kernel(**inputs):
    import numpy as _np
    import concourse.bacc as _bacc
    from concourse import mybir as _mybir
    from concourse.bass_utils import run_bass_kernel_spmd as _run

    nc = _bacc.Bacc("TRN2", target_bir_lowering=False, num_devices=1)
    arrays, args = {}, []
    for name in _INS:
        a = _np.ascontiguousarray(inputs[name])
        arrays[f"in_{name}_dram"] = a
        args.append(nc.dram_tensor(f"in_{name}_dram", a.shape, _mybir.dt.from_np(a.dtype),
                                   kind="ExternalInput").ap())
    shape = _np.asarray(inputs['x']).shape
    args.append(nc.dram_tensor("out_0_dram", shape, _mybir.dt.float32, kind="ExternalOutput").ap())
    gated_graph_net(nc, *args)
    r = _run(nc, [arrays], core_ids=[0])
    return r.results[0]["out_0_dram"]
```
